# Optimizing a Trainium2 kernel written in Bass

```python
import numpy as np
import jax
import jax.numpy as jnp

def _softmax(x, axis=-1):
    return jax.nn.softmax(x, axis=axis)

def _gelu(x):
    return jax.nn.gelu(x, approximate=True)

def _silu(x):
    return jax.nn.silu(x)

def _sigmoid(x):
    return jax.nn.sigmoid(x)

def _layernorm(x, axis=-1, eps=1e-05):
    m = jnp.mean(x, axis=axis, keepdims=True)
    v = jnp.var(x, axis=axis, keepdims=True)
    return (x - m) / jnp.sqrt(v + eps)

def _scatter_add(tgt, idx, src, axis=0):
    return tgt.at[idx].add(src)

def _segment_sum(src, seg, n):
    return jax.ops.segment_sum(src, seg, n)
kernel_name = 'mk_seq_postln_d1_jaxref_r4_6c9aba'

def setup_inputs(seed: int=0):
    np.random.seed(seed)
    _w = jnp.asarray

    def _L0_attn_setup():
        import jax, jax.numpy as jnp
        import numpy as np
        D_MODEL = 256
        N_HEADS = 16
        N_GROUPS = 4
        CONTEXT_LEN = 128
        D_H = D_MODEL // N_HEADS
        GROUP_SIZE = N_HEADS // N_GROUPS
        B, S = (4, 512)
        key = jax.random.key(seed)
        ks = jax.random.split(key, 9)
        s = 0.02
        return {'x': jax.random.normal(ks[0], (B, S, D_MODEL), dtype=jnp.float32), 'Wq': jax.random.normal(ks[1], (D_MODEL, D_MODEL), dtype=jnp.float32) * s, 'bq': jax.random.normal(ks[2], (D_MODEL,), dtype=jnp.float32) * s, 'Wk': jax.random.normal(ks[3], (D_MODEL, N_GROUPS * D_H), dtype=jnp.float32) * s, 'bk': jax.random.normal(ks[4], (N_GROUPS * D_H,), dtype=jnp.float32) * s, 'Wv': jax.random.normal(ks[5], (D_MODEL, N_GROUPS * D_H), dtype=jnp.float32) * s, 'bv': jax.random.normal(ks[6], (N_GROUPS * D_H,), dtype=jnp.float32) * s, 'Wo': jax.random.normal(ks[7], (D_MODEL, D_MODEL), dtype=jnp.float32) * s, 'bo': jax.random.normal(ks[8], (D_MODEL,), dtype=jnp.float32) * s}
    _L0_attn_in = _L0_attn_setup()

    def _L0_ffn_setup():
        import jax, jax.numpy as jnp
        import numpy as np
        DIM = 256

        def _reference_tuple_inner(x, W_r, W_k, W_v, mu_r, mu_k):
            B, T, C = x.shape
            x_prev = jnp.concatenate([jnp.zeros((B, 1, C), x.dtype), x[:, :-1, :]], axis=1)
            xr = mu_r * x + (1.0 - mu_r) * x_prev
            xk = mu_k * x + (1.0 - mu_k) * x_prev
            r = jax.nn.sigmoid(jnp.einsum('btc,dc->btd', xr, W_r))
            k = jnp.einsum('btc,dc->btd', xk, W_k)
            k_act = jnp.square(jax.nn.relu(k))
            out = r * jnp.einsum('btc,dc->btd', k_act, W_v)
            new_state = x[:, -1, :]
            return (out, new_state)
        key = jax.random.key(seed)
        ks = jax.random.split(key, 6)
        B, T, C = (8, 512, DIM)
        x = jax.random.normal(ks[0], (B, T, C), dtype=jnp.float32)
        s = 1.0 / np.sqrt(C)
        W_r = jax.random.uniform(ks[1], (C, C), jnp.float32, -s, s)
        W_k = jax.random.uniform(ks[2], (C, C), jnp.float32, -s, s)
        W_v = jax.random.uniform(ks[3], (C, C), jnp.float32, -s, s)
        mu_r = jax.random.uniform(ks[4], (C,), jnp.float32)
        mu_k = jax.random.uniform(ks[5], (C,), jnp.float32)
        return {'x': x, 'W_r': W_r, 'W_k': W_k, 'W_v': W_v, 'mu_r': mu_r, 'mu_k': mu_k}
    _L0_ffn_in = _L0_ffn_setup()
    _d = {'L0_attn_x': _L0_attn_in['x'], 'L0_attn_Wq': _L0_attn_in['Wq'], 'L0_attn_bq': _L0_attn_in['bq'], 'L0_attn_Wk': _L0_attn_in['Wk'], 'L0_attn_bk': _L0_attn_in['bk'], 'L0_attn_Wv': _L0_attn_in['Wv'], 'L0_attn_bv': _L0_attn_in['bv'], 'L0_attn_Wo': _L0_attn_in['Wo'], 'L0_attn_bo': _L0_attn_in['bo'], 'L0_ffn_W_r': _L0_ffn_in['W_r'], 'L0_ffn_W_k': _L0_ffn_in['W_k'], 'L0_ffn_W_v': _L0_ffn_in['W_v'], 'L0_ffn_mu_r': _L0_ffn_in['mu_r'], 'L0_ffn_mu_k': _L0_ffn_in['mu_k']}
    _x0 = _d['L0_attn_x']
    _d['L0_attn_x'] = jax.random.normal(jax.random.fold_in(jax.random.key(seed), 1), (1, 4096, 256), dtype=_x0.dtype)
    del _x0
    return _d

def reference(L0_attn_x, L0_attn_Wq, L0_attn_bq, L0_attn_Wk, L0_attn_bk, L0_attn_Wv, L0_attn_bv, L0_attn_Wo, L0_attn_bo, L0_ffn_W_r, L0_ffn_W_k, L0_ffn_W_v, L0_ffn_mu_r, L0_ffn_mu_k):

    def _L0_attn_ref(x, Wq, bq, Wk, bk, Wv, bv, Wo, bo):
        import jax, jax.numpy as jnp
        import numpy as np
        D_MODEL = 256
        N_HEADS = 16
        N_GROUPS = 4
        CONTEXT_LEN = 128
        D_H = D_MODEL // N_HEADS
        GROUP_SIZE = N_HEADS // N_GROUPS
        B, S = (4, 512)
        b, s = (x.shape[0], x.shape[1])
        q = (x @ Wq + bq).reshape(b, s, N_GROUPS, GROUP_SIZE, D_H)
        q = jnp.transpose(q, (0, 2, 3, 1, 4))
        k = jnp.transpose((x @ Wk + bk).reshape(b, s, N_GROUPS, D_H), (0, 2, 1, 3))
        v = jnp.transpose((x @ Wv + bv).reshape(b, s, N_GROUPS, D_H), (0, 2, 1, 3))
        scores = jnp.einsum('bghqd,bgkd->bghqk', q, k) / jnp.sqrt(jnp.float32(D_H))
        i = jnp.arange(s)
        j = jnp.arange(s)
        upper = (i - CONTEXT_LEN)[:, None] >= j[None, :]
        lower = i[:, None] < j[None, :]
        mask = upper | lower
        scores = jnp.where(mask, jnp.float32(-1000000000.0), scores)
        att = jax.nn.softmax(scores, axis=-1)
        out = jnp.einsum('bghqk,bgkd->bghqd', att, v)
        out = jnp.transpose(out, (0, 3, 1, 2, 4)).reshape(b, s, D_MODEL)
        return out @ Wo + bo

    def _L0_ffn_ref(x, W_r, W_k, W_v, mu_r, mu_k):
        import jax, jax.numpy as jnp
        import numpy as np
        DIM = 256

        def _reference_tuple_inner(x, W_r, W_k, W_v, mu_r, mu_k):
            B, T, C = x.shape
            x_prev = jnp.concatenate([jnp.zeros((B, 1, C), x.dtype), x[:, :-1, :]], axis=1)
            xr = mu_r * x + (1.0 - mu_r) * x_prev
            xk = mu_k * x + (1.0 - mu_k) * x_prev
            r = jax.nn.sigmoid(jnp.einsum('btc,dc->btd', xr, W_r))
            k = jnp.einsum('btc,dc->btd', xk, W_k)
            k_act = jnp.square(jax.nn.relu(k))
            out = r * jnp.einsum('btc,dc->btd', k_act, W_v)
            new_state = x[:, -1, :]
            return (out, new_state)
        return _reference_tuple_inner(x, W_r, W_k, W_v, mu_r, mu_k)[0]
    x = L0_attn_x
    x = _layernorm(x + _L0_attn_ref(x, L0_attn_Wq, L0_attn_bq, L0_attn_Wk, L0_attn_bk, L0_attn_Wv, L0_attn_bv, L0_attn_Wo, L0_attn_bo), axis=-1)
    x = _layernorm(x + _L0_ffn_ref(x, L0_ffn_W_r, L0_ffn_W_k, L0_ffn_W_v, L0_ffn_mu_r, L0_ffn_mu_k), axis=-1)
    return x

_drawn_inputs = setup_inputs


def setup_inputs(seed=0):
    import zlib

    import numpy as np

    out = dict(_drawn_inputs(seed))
    spreads = {}
    factors = {'L0_attn_Wq': 8.0,
     'L0_attn_bq': 8.0,
     'L0_attn_Wk': 8.0,
     'L0_attn_bk': 8.0,
     'L0_attn_Wv': 5.693,
     'L0_attn_bv': 8.0,
     'L0_attn_Wo': 4.586,
     'L0_attn_bo': 2.925,
     'L0_ffn_W_r': 3.18,
     'L0_ffn_mu_r': 6.398}
    for name, (base, spread) in spreads.items():
        noise = np.random.default_rng([zlib.crc32(name.encode()), seed]).standard_normal(out[name].shape)
        drawn = base * np.exp(spread * noise) if base else spread * noise
        out[name] = jnp.asarray(drawn.astype(out[name].dtype))
    for name, factor in factors.items():
        out[name] = (out[name] * factor).astype(out[name].dtype)
    return out
```

```python
from contextlib import ExitStack

import concourse.bass as bass
from concourse import mybir

F32 = mybir.dt.float32
BF16 = mybir.dt.bfloat16
ALU = mybir.AluOpType
ACT = mybir.ActivationFunctionType
AX_X = mybir.AxisListType.X

P = 128
HEADS = 16
GROUPS = 4
HPG = HEADS // GROUPS
WINDOW = 128
BLK = 128
SUB = 32
NSUB = BLK // SUB
TILE_KEYS = WINDOW + SUB
SB_BLKS = 4
SB = SB_BLKS * BLK
NTILE = GROUPS * NSUB
TPB = 3
NMAXB = -(-NTILE // TPB)
NSCORE = 2 * GROUPS
PARTS = 3
Q_PART = (0, 0, 0, 1, 1, 2)
K_PART = (0, 1, 2, 0, 1, 0)
NREP = len(Q_PART)
VCOL = 32
MASKED = -1e30
EPS = 1e-5


def attention_channel_mix(nc, x, Wq, bq, Wk, bk, Wv, bv, Wo, bo, W_r, W_k, W_v, mu_r, mu_k, out):
    S, D = x.shape[1], x.shape[2]
    DH = D // HEADS
    DKV = GROUPS * DH
    DC = D // P
    NBLK = S // BLK
    NSB = S // SB
    QCH = D // P
    NCH = QCH + 1
    ROWS = NREP * DH
    SCALE = float(DH) ** -0.5
    assert 2 * DKV == P and ROWS == 96 and NBLK % SB_BLKS == 0 and NSB % 2 == 0

    assert QCH * 2 == HPG and GROUPS * SUB == BLK
    x_sb = x.rearrange("b (s j p) d -> (b s) p j d", j=SB_BLKS, p=BLK)
    out_blk = out.rearrange("b (t p) d -> (b t) p d", p=BLK)

    q_dram = nc.dram_tensor("q_parts", [2, PARTS, SB_BLKS, QCH, P, BLK], BF16, kind="Internal").ap()
    k_dram = nc.dram_tensor("k_parts", [PARTS, DKV, S], BF16, kind="Internal").ap()

    SPILLS = 16 * (PARTS * QCH + 1)
    STACKS = 16 * 2 * NREP
    MAX_IN = 16 * HPG
    N_CONST = 8
    N_SMALL = 16 * (QCH * P // DH + 7)

    with ExitStack() as ctx:
        def sb(name, shape, dt=F32):
            return ctx.enter_context(nc.sbuf_tensor(name, shape, dt))

        def bank(name, dt=F32):
            return ctx.enter_context(nc.psum_tensor(name, [P, 512], dt))

        def sem(name):
            return ctx.enter_context(nc.semaphore(name))

        ident = sb("ident", [P, P])
        ident_b = sb("ident_b", [P, P], BF16)
        edge_f = sb("edge_f", [P, 2, SUB])
        edge_mask = sb("edge_mask", [P, TPB, 2, SUB], BF16)
        first_f = sb("first_f", [P, NSUB, TILE_KEYS])
        first_mask = sb("first_mask", [P, NSUB, TILE_KEYS], BF16)
        wq_raw = sb("wq_raw", [P, DC, D])
        wqkv = sb("wqkv", [P, DC, D + 2 * DKV])
        wo = sb("wo", [P, DC, D])
        w_raw = sb("w_raw", [P, 3, DC, D])
        w_t = sb("w_t", [P, 3, DC, D])
        bias_qkv = sb("bias_qkv", [P, NCH])
        bo_b = sb("bo_b", [P, D])
        mu = sb("mu", [P, 2, DC])
        minus_half = sb("minus_half", [P, 1])
        x_in = sb("x_in", [P, SB_BLKS, D])
        x_bo = sb("x_bo", [P, 2, SB_BLKS, D])
        x_t = sb("x_t", [P, DC, SB])
        proj = sb("proj", [P, NCH, SB])
        rest = sb("rest", [P, NCH, SB])
        parts = sb("parts", [P, NCH, PARTS, SB], BF16)
        qs = sb("qs", [P, 2, SB_BLKS, HPG, GROUPS, BLK], BF16)
        ks = sb("ks", [P, 2, GROUPS, WINDOW + SB], BF16)
        vals = sb("vals", [P, 2, SB_BLKS, GROUPS, VCOL])
        q_tiles = sb("q_tiles", [ROWS, 2, NTILE, HPG * SUB], BF16)
        neg_max = sb("neg_max", [P, NTILE])
        max_rest = sb("max_rest", [P, NTILE])
        max_parts = sb("max_parts", [P, 2, PARTS, NTILE], BF16)
        max_rows = sb("max_rows", [P, 2, P], BF16)
        probs = sb("probs", [P, 2, NSCORE, HPG * BLK])
        att_t = sb("att_t", [P, HPG * BLK])
        recip = sb("recip", [P, HEADS])
        att = sb("att", [P, D])
        att_c = sb("att_c", [P, DC, BLK])
        y1 = sb("y1", [P, D])
        stats1 = sb("stats1", [P, 6])
        mv1 = sb("mv1", [P, 2])
        var1 = sb("var1", [P, 1])
        rstd1 = sb("rstd1", [P, 1])
        x2 = sb("x2", [P, 2, D])
        x2_t = sb("x2_t", [P, 2, DC, 1 + BLK])
        diff = sb("diff", [P, DC, BLK])
        mix = sb("mix", [P, 2, DC, BLK])
        tanh_r = sb("tanh_r", [P, D])
        relu_k = sb("relu_k", [P, DC, BLK])
        act_k = sb("act_k", [P, DC, BLK])
        gated = sb("gated", [P, D])
        y2 = sb("y2", [P, D])
        stats2 = sb("stats2", [P, 6])
        mv2 = sb("mv2", [P, 2])
        var2 = sb("var2", [P, 1])
        rstd2 = sb("rstd2", [P, 1])
        out_t = sb("out_t", [P, 2, D])

        max_ps = [bank(f"max_ps{i}") for i in range(2)]
        score_ps = [bank(f"score_ps{i}") for i in range(2)]
        av_ps = bank("av_ps")
        gen0 = bank("gen0")
        gen1 = bank("gen1")
        proj_ps = bank("proj_ps")

        s_ident = sem("s_ident")
        s_const = sem("s_const")
        s_edge = sem("s_edge")
        s_masks = sem("s_masks")
        s_zero = sem("s_zero")
        s_wqkv = sem("s_wqkv")
        s_wo = sem("s_wo")
        s_wffn = sem("s_wffn")
        s_small = sem("s_small")
        s_wtr = sem("s_wtr")
        s_wcp = sem("s_wcp")
        s_x = sem("s_x")
        s_xbo = sem("s_xbo")
        s_xtr = sem("s_xtr")
        s_xt = sem("s_xt")
        s_proj = sem("s_proj")
        s_pcp = sem("s_pcp")
        s_vtr = sem("s_vtr")
        s_val = sem("s_val")
        s_hi = sem("s_hi")
        s_rest = sem("s_rest")
        s_mid = sem("s_mid")
        s_lo = sem("s_lo")
        s_spill = sem("s_spill")
        s_stack = sem("s_stack")
        s_tiles = sem("s_tiles")
        s_maxsc = sem("s_maxsc")
        s_max = sem("s_max")
        s_mx = sem("s_mx")
        s_maxtr = sem("s_maxtr")
        s_maxrow = sem("s_maxrow")
        s_maxin = sem("s_maxin")
        s_score = sem("s_score")
        s_exp = sem("s_exp")
        s_prob = sem("s_prob")
        s_av = sem("s_av")
        s_att_t = sem("s_att_t")
        s_atr = sem("s_atr")
        s_recip = sem("s_recip")
        s_att = sem("s_att")
        s_ctr = sem("s_ctr")
        s_att_c = sem("s_att_c")
        s_wo_ps = sem("s_wo_ps")
        s_y1 = sem("s_y1")
        s_ln1 = sem("s_ln1")
        s_rstd1 = sem("s_rstd1")
        s_x2 = sem("s_x2")
        s_x2tr = sem("s_x2tr")
        s_x2t = sem("s_x2t")
        s_x2p = sem("s_x2p")
        s_diff = sem("s_diff")
        s_mix = sem("s_mix")
        s_r = sem("s_r")
        s_k = sem("s_k")
        s_tanh = sem("s_tanh")
        s_relu = sem("s_relu")
        s_act_k = sem("s_act_k")
        s_v = sem("s_v")
        s_gated = sem("s_gated")
        s_y2 = sem("s_y2")
        s_ln2 = sem("s_ln2")
        s_rstd2 = sem("s_rstd2")
        s_wqp = sem("s_wqp")
        s_out = sem("s_out")
        s_store = [sem("s_store0"), sem("s_store1")]

        def later(t, n):
            return not isinstance(t, int) or t >= n

        def at(j, par, d):
            return (j + d) % SB_BLKS, par ^ ((j + d) // SB_BLKS & 1)

        def stored(s, j):
            return s * (16 * SB_BLKS // 2) + 16 * ((j - 5) // 2 + 1) + 1

        def scored(t, i):
            if isinstance(t, int) and t == 0:
                return i // 2 + 1
            return t * NSCORE - NSCORE // 2 + i + 1

        block = ctx.enter_context(nc.Block())

        def run(eng, start, step, tail=None):
            def superblock(s, par, last=False):
                for j in range(SB_BLKS):
                    step(s, j, par, project=not last, maxima=not last or j < SB_BLKS - 1, scores=True)

            start()
            superblock(0, 0)
            with eng.Fori(0, (NSB - 2) // 2) as pair:
                superblock(pair * 2 + 1, 1)
                superblock(pair * 2 + 2, 0)
            superblock(NSB - 1, 1, last=True)
            for j in range(SB_BLKS, SB_BLKS + 3):
                step(NSB - 1, j, 1, project=False, maxima=False, scores=False)
            if tail:
                tail()

        def behind(t, j, scores, n):
            return later(t, n) and (scores or j - n < SB_BLKS)

        @block.sync
        def _(sp):
            def load_x(s):
                sp.dma_start(x_in[:, :, :], x_sb[s]).then_inc(s_x, 16)

            def spill_q(s, par, m):
                sp.wait_ge(s_lo, s * NCH + m + 1)
                sp.nop(nofuse=True)
                for a in range(PARTS):
                    sp.dma_start(q_dram[par, a, :, m].rearrange("j p t -> p j t"),
                                 parts[:, m, a, :].rearrange("p (j t) -> p j t", t=BLK)).then_inc(s_spill, 16)

            def spill_k(s):
                sp.wait_ge(s_lo, s * NCH + NCH)
                sp.nop(nofuse=True)
                sp.dma_start(k_dram[:, :, bass.ds(s * SB, SB)].rearrange("a p t -> p a t"),
                             parts[0:DKV, QCH]).then_inc(s_spill, 16)

            def stack_q(s, par, rep):
                if rep == 0:
                    sp.wait_ge(s_spill, s * SPILLS + 16 * PARTS * QCH)
                    sp.nop(nofuse=True)
                    if later(s, 2):
                        sp.wait_ge(s_score, scored(s * SB_BLKS - SB_BLKS - 1, NSCORE - 1))
                        sp.nop(nofuse=True)
                sp.dma_start(qs[rep * DH:(rep + 1) * DH, par].rearrange("d j (m x) g t -> d (j m) (x g t)", m=QCH),
                             q_dram[par, Q_PART[rep]].rearrange("j m (d y) t -> d (j m) (y t)", d=DH)
                             ).then_inc(s_stack, 16)

            def stack_k(s, par, rep):
                if rep == 0:
                    sp.wait_ge(s_spill, s * SPILLS + SPILLS)
                    sp.nop(nofuse=True)
                src = k_dram[K_PART[rep]].rearrange("(g d) t -> d g t", d=DH)
                if not later(s, 1):
                    sp.dma_start(ks[rep * DH:(rep + 1) * DH, par, :, WINDOW:], src[:, :, 0:SB]).then_inc(s_stack, 16)
                else:
                    sp.dma_start(ks[rep * DH:(rep + 1) * DH, par],
                                 src[:, :, bass.ds(s * SB - WINDOW, WINDOW + SB)]).then_inc(s_stack, 16)

            def max_in(t, j, par):
                sp.wait_ge(s_maxrow, t + 1)
                sp.nop(nofuse=True)
                for h in range(HPG):
                    sp.dma_start(qs[ROWS:ROWS + PARTS, par, j, h].rearrange("a g t -> a (g t)"),
                                 max_rows[0:PARTS * NTILE, j % 2, h * SUB:(h + 1) * SUB]).then_inc(s_maxin, 16)

            def store(t, buf):
                sp.wait_ge(s_out, t + 1)
                sp.nop(nofuse=True)
                sp.dma_start(out_blk[t], out_t[:, buf]).then_inc(s_store[buf], 16)

            def start():
                load_x(0)
                sp.dma_start(wq_raw[:, :, :], Wq.rearrange("(c p) n -> p c n", p=P)).then_inc(s_wqkv, 16)
                sp.dma_start(wqkv[:, :, D:D + DKV], Wk.rearrange("(c p) n -> p c n", p=P)).then_inc(s_wqkv, 16)
                sp.dma_start(wqkv[:, :, D + DKV:], Wv.rearrange("(c p) n -> p c n", p=P)).then_inc(s_wqkv, 16)
                sp.dma_start(wo[:, :, :], Wo.rearrange("(c p) n -> p c n", p=P)).then_inc(s_wo, 16)
                for n, w in enumerate((W_r, W_k, W_v)):
                    sp.dma_start(w_raw[:, n], w.rearrange("(c p) n -> p c n", p=P)).then_inc(s_wffn, 16)
                sp.wait_ge(s_const, N_CONST)
                sp.nop(nofuse=True)
                for h in range(1, HPG):
                    sp.dma_start(edge_f[h * SUB:(h + 1) * SUB], edge_f[0:SUB]).then_inc(s_edge, 16)
                    sp.dma_start(first_f[h * SUB:(h + 1) * SUB], first_f[0:SUB]).then_inc(s_edge, 16)
                for m in range(QCH):
                    spill_q(0, 0, m)
                for rep in range(NREP):
                    stack_q(0, 0, rep)
                spill_k(0)
                for rep in range(NREP):
                    stack_k(0, 0, rep)
                max_in(0, 0, 0)

            def step(s, j, par, project, maxima, scores):
                t = s * SB_BLKS + j
                if project and j == 0:
                    sp.wait_ge(s_xtr, s * DC + DC)
                    sp.nop(nofuse=True)
                    sp.wait_ge(s_xbo, s + 1)
                    sp.nop(nofuse=True)
                    load_x(s + 1)
                if project and j == 1:
                    for m in range(QCH):
                        spill_q(s + 1, 1 - par, m)
                    for rep in range(2):
                        stack_q(s + 1, 1 - par, rep)
                if project and j == 2:
                    for rep in range(3):
                        stack_k(s + 1, 1 - par, rep)
                if maxima:
                    max_in(t + 1, *at(j, par, 1))
                if behind(t, j, scores, 3):
                    store(t - 3, (j - 3) % 2)
                if project and j == 1:
                    for rep in range(2, NREP):
                        stack_q(s + 1, 1 - par, rep)
                    spill_k(s + 1)
                if project and j == 2:
                    for rep in range(3, NREP):
                        stack_k(s + 1, 1 - par, rep)

            def tail():
                for buf in range(2):
                    sp.wait_ge(s_store[buf], 16 * (NBLK // 2) + 1)
                    sp.nop(nofuse=True)

            run(sp, start, step, tail)

        @block.gpsimd
        def _(pool):
            def x_plus_bo(s, par):
                pool.wait_ge(s_x, s * 16 + 16)
                nc.gpsimd.tensor_tensor(x_bo[:, par], x_in[:, :, :],
                                        bo_b[:, :].unsqueeze(1).to_broadcast([P, SB_BLKS, D]), ALU.add).then_inc(s_xbo, 1)

            def rest_of(s, m):
                pool.wait_ge(s_hi, s * NCH + m + 1)
                nc.gpsimd.tensor_tensor(rest[:, m], proj[:, m], parts[:, m, 0], ALU.subtract).then_inc(s_rest, 1)

            def mask(t, i, buf):
                pool.wait_ge(s_exp, scored(t, i))
                pool.nop(nofuse=True)
                v = probs[:, buf, i].rearrange("p (h q) -> p h q", q=BLK)
                sign = 1 if i % 2 else -1
                nc.gpsimd.affine_select(out=v, in_=v, compare_op=ALU.is_ge if i % 2 else ALU.is_gt, fill=0.0,
                                        base=0, pattern=[[0, HPG], [sign, BLK]],
                                        channel_multiplier=-sign).then_inc(s_prob, 1)

            def rstd(u, var, out_, ready, steps, done):
                pool.wait_ge(ready, u * steps + steps)
                nc.gpsimd.tensor_tensor(out_[:, :], var[:, :], minus_half[:, :], ALU.pow).then_inc(done, 1)

            def start():
                nc.gpsimd.memset(ident[:, :], 0.0).then_inc(s_const, 1)
                nc.gpsimd.memset(edge_f[0:SUB], 0.0).then_inc(s_const, 1)
                nc.gpsimd.memset(first_f[0:SUB], 0.0).then_inc(s_const, 1)
                nc.gpsimd.memset(minus_half[:, :], -0.5).then_inc(s_const, 1)
                pool.wait_ge(s_const, 4)
                nc.gpsimd.affine_select(out=ident[:, :], in_=ident[:, :], compare_op=ALU.not_equal, fill=1.0, base=0,
                                        pattern=[[-1, P]], channel_multiplier=1).then_inc(s_ident, 1)
                nc.gpsimd.affine_select(out=edge_f[0:SUB, 0], in_=edge_f[0:SUB, 0], compare_op=ALU.is_gt, fill=MASKED,
                                        base=0, pattern=[[1, SUB]], channel_multiplier=-1).then_inc(s_const, 1)
                nc.gpsimd.affine_select(out=edge_f[0:SUB, 1], in_=edge_f[0:SUB, 1], compare_op=ALU.is_ge, fill=MASKED,
                                        base=0, pattern=[[-1, SUB]], channel_multiplier=1).then_inc(s_const, 1)
                nc.gpsimd.affine_select(out=first_f[0:SUB], in_=first_f[0:SUB], compare_op=ALU.is_ge, fill=MASKED,
                                        base=-WINDOW, pattern=[[SUB, NSUB], [1, TILE_KEYS]],
                                        channel_multiplier=0).then_inc(s_const, 1)
                pool.wait_ge(s_const, 7)
                nc.gpsimd.affine_select(out=first_f[0:SUB, :, WINDOW:], in_=first_f[0:SUB, :, WINDOW:],
                                        compare_op=ALU.is_ge, fill=MASKED, base=0, pattern=[[0, NSUB], [-1, SUB]],
                                        channel_multiplier=1).then_inc(s_const, 1)
                pool.wait_ge(s_small, N_SMALL)
                x_plus_bo(0, 0)
                for m in range(NCH):
                    rest_of(0, m)

            def step(s, j, par, project, maxima, scores):
                t = s * SB_BLKS + j
                f2, f3 = (behind(t, j, scores, n) for n in (2, 3))
                if f2:
                    rstd(t - 2, var1, rstd1, s_ln1, 3, s_rstd1)
                for i in range(NSCORE):
                    if i == 2 and f3:
                        rstd(t - 3, var2, rstd2, s_ln2, 3, s_rstd2)
                    if scores and (i % 2 or later(t, 1)):
                        mask(t, i, j % 2)
                    if i == 3 and f2:
                        u2 = (j - 2) % 2
                        pool.wait_ge(s_x2t, t - 1)
                        if later(t, 3):
                            pool.wait_ge(s_x2p, t - 2)
                        nc.gpsimd.tensor_tensor(diff[:, :, :], x2_t[:, u2, :, 1:], x2_t[:, u2, :, 0:BLK],
                                                ALU.subtract).then_inc(s_diff, 1)
                    if i == 7 and f2:
                        pool.wait_ge(s_relu, t - 1)
                        nc.gpsimd.tensor_tensor(act_k[:, :, :], relu_k[:, :, :], relu_k[:, :, :],
                                                ALU.mult).then_inc(s_act_k, 1)
                    if project and j == 0 and i >= 5:
                        rest_of(s + 1, i - 5)
                    if project and j == 2 and i == 0:
                        if later(s, 1):
                            pool.wait_ge(s_y1, s * SB_BLKS)
                        x_plus_bo(s + 1, 1 - par)

            run(pool, start, step)

        @block.scalar
        def _(act):
            def x_t_copy(s, c):
                act.wait_ge(s_xtr, s * DC + c + 1)
                if later(s, 1):
                    act.wait_ge(s_proj, s * NCH)
                nc.scalar.copy(x_t[:, c], proj_ps[:, 0:SB]).then_inc(s_xt, 1)

            def proj_copy(s, m):
                act.wait_ge(s_proj, s * NCH + m + 1)
                if later(s, 1):
                    act.wait_ge(s_lo, s * NCH - NCH + m + 1)
                    if m == QCH:
                        act.wait_ge(s_vtr, s)
                nc.scalar.activation(proj[:, m], proj_ps[:, 0:SB], ACT.Identity,
                                     bias=bias_qkv[:, m:m + 1]).then_inc(s_pcp, 1)

            def max_row_copy(t, j):
                act.wait_ge(s_maxtr, t + 1)
                if later(t, 2):
                    act.wait_ge(s_maxin, t * MAX_IN - MAX_IN)
                nc.scalar.copy(max_rows[0:PARTS * NTILE, j % 2],
                               max_ps[0][0:PARTS * NTILE, 0:P // 2].bitcast(BF16)).then_inc(s_maxrow, 1)

            def exps(t, i, buf):
                act.wait_ge(s_score, scored(t, i))
                if i <= 1 and later(t, 2):
                    act.wait_ge(s_av, t - 1)
                nc.scalar.activation(probs[:, buf, i], score_ps[i % 2][:, :], ACT.Exp, scale=SCALE).then_inc(s_exp, 1)

            def start():
                bq_v = bq.rearrange("(g m h d o) -> m h g d o", g=GROUPS, m=QCH, d=DH, o=1)
                step_d = P // DH
                for m in range(QCH):
                    for hg in range(step_d):
                        act.dma_start(bias_qkv[hg:hg + step_d * (DH - 1) + 1:step_d, m:m + 1],
                                      bq_v[m, hg // GROUPS, hg % GROUPS]).then_inc(s_small, 16)
                act.dma_start(bias_qkv[0:DKV, QCH:], bk.rearrange("(p c) -> p c", c=1)).then_inc(s_small, 16)
                act.dma_start(bias_qkv[DKV:P, QCH:], bv.rearrange("(p c) -> p c", c=1)).then_inc(s_small, 16)
                for w, vec in enumerate((mu_r, mu_k)):
                    for c in range(DC):
                        act.dma_start(mu[:, w, c:c + 1], vec[c * P:(c + 1) * P].rearrange("(p o) -> p o", o=1)).then_inc(s_small, 16)
                
                act.dma_start(bo_b[:, :], bo.rearrange("(o n) -> o n", o=1).to_broadcast([P, D])).then_inc(s_small, 16)
                x_t_copy(0, 0)
                x_t_copy(0, 1)
                act.wait_ge(s_small, N_SMALL)
                for m in range(NCH):
                    proj_copy(0, m)
                for n in range(3):
                    for c in range(DC):
                        act.wait_ge(s_wtr, DC * n + c + 1)
                        nc.scalar.copy(w_t[:, n, c], (gen0, gen1)[c][:, 0:D]).then_inc(s_wcp, 1)
                max_row_copy(0, 0)

            def step(s, j, par, project, maxima, scores):
                t = s * SB_BLKS + j
                f1, f2 = (behind(t, j, scores, n) for n in (1, 2))
                for i in range(NSCORE):
                    if scores and (i % 2 or later(t, 1)):
                        exps(t, i, j % 2)
                    if i == 2 and f1:
                        act.wait_ge(s_av, t)
                        nc.scalar.copy(att_t[:, :], av_ps[:, :]).then_inc(s_att_t, 1)
                    if i == 2 and f2:
                        act.wait_ge(s_x2tr, t - 1)
                        if later(t, 4):
                            act.wait_ge(s_mix, (t - 3) * 4)
                        nc.scalar.copy(x2_t[:, (j - 2) % 2, :, 1:],
                                       gen0[:, 0:DC * BLK].rearrange("p (c q) -> p c q", q=BLK)).then_inc(s_x2t, 1)
                    if project and j == 0 and i in (2, 3):
                        x_t_copy(s + 1, i - 2)
                    if i == 4 and maxima:
                        max_row_copy(t + 1, j + 1)
                    if project and j == 0 and i in (4, 5, 6):
                        proj_copy(s + 1, i - 4)
                    if i == 5 and f1:
                        act.wait_ge(s_ctr, t)
                        nc.scalar.copy(att_c[:, :, :],
                                       gen0[:, 0:D].rearrange("p (c q) -> p c q", q=BLK)).then_inc(s_att_c, 1)
                    if i == 5 and f2:
                        act.wait_ge(s_r, t - 1)
                        nc.scalar.activation(tanh_r[:, :], gen1[:, 0:D], ACT.Tanh, scale=0.5).then_inc(s_tanh, 1)
                    if i == 6 and f2:
                        act.wait_ge(s_k, t - 1)
                        nc.scalar.activation(relu_k[:, :, :], gen0[:, 0:DC * BLK].rearrange("p (c q) -> p c q", q=BLK),
                                             ACT.Relu).then_inc(s_relu, 1)

            run(act, start, step)

        @block.vector
        def _(dve):
            def hi(s, m):
                dve.wait_ge(s_pcp, s * NCH + m + 1)
                if later(s, 1):
                    dve.wait_ge(s_spill, s * SPILLS)
                nc.vector.tensor_copy(parts[:, m, 0], proj[:, m]).then_inc(s_hi, 1)

            def mid_lo(s, m):
                dve.wait_ge(s_rest, s * NCH + m + 1)
                nc.vector.tensor_copy(parts[:, m, 1], rest[:, m]).then_inc(s_mid, 1)
                dve.wait_ge(s_mid, s * NCH + m + 1)
                nc.vector.tensor_tensor(parts[:, m, 2], rest[:, m], parts[:, m, 1], ALU.subtract).then_inc(s_lo, 1)

            def val_copy(s, par):
                dve.wait_ge(s_vtr, s + 1)
                if later(s, 2):
                    dve.wait_ge(s_av, s * SB_BLKS - 3)
                nc.vector.tensor_copy(vals[:, par, :, :, 0:DH],
                                      proj_ps[:, 0:SB].rearrange("p (j x g d) -> p j x g d", x=2, g=GROUPS, d=DH)[:, :, 1]
                                      ).then_inc(s_val, 1)

            def tile_q(t, s, j, par):
                if j == 0:
                    dve.wait_ge(s_stack, s * STACKS + STACKS)
                nc.vector.tensor_copy(q_tiles[:, j % 2].rearrange("r n (h q) -> r n h q", q=SUB),
                                      qs[0:ROWS, par, j].rearrange("r h g (n q) -> r (g n) h q", q=SUB)
                                      ).then_inc(s_tiles, 1)

            def tile_max(t, i):
                n = min(TPB, NTILE - TPB * i)
                dve.wait_ge(s_maxsc, t * NMAXB + i + 1)
                nc.vector.tensor_reduce(neg_max[:, TPB * i:TPB * i + n],
                                        max_ps[i % 2][:, 0:n * TILE_KEYS].rearrange("p (n k) -> p n k", k=TILE_KEYS),
                                        AX_X, ALU.max, negate=True).then_inc(s_max, 1)

            def cut_max(t, j):
                mp = max_parts[:, j % 2]
                dve.wait_ge(s_max, t * NMAXB + NMAXB)
                nc.vector.tensor_copy(mp[:, 0], neg_max[:, :]).then_inc(s_mx, 1)
                dve.wait_ge(s_mx, t * 4 + 1)
                nc.vector.tensor_tensor(max_rest[:, :], neg_max[:, :], mp[:, 0], ALU.subtract).then_inc(s_mx, 1)
                dve.wait_ge(s_mx, t * 4 + 2)
                nc.vector.tensor_copy(mp[:, 1], max_rest[:, :]).then_inc(s_mx, 1)
                dve.wait_ge(s_mx, t * 4 + 3)
                nc.vector.tensor_tensor(mp[:, 2], max_rest[:, :], mp[:, 1], ALU.subtract).then_inc(s_mx, 1)

            def moments(u, y, y_done, stats, mv, var, done):
                dve.wait_ge(y_done, u + 1)
                nc.vector.bn_stats(stats[:, :], y[:, :]).then_inc(done, 1)
                dve.wait_ge(done, u * 3 + 1)
                dve.nop(nofuse=True)
                nc.vector.bn_aggr(mv[:, :], stats[:, :]).then_inc(done, 1)
                dve.wait_ge(done, u * 3 + 2)
                nc.vector.tensor_scalar(var[:, :], mv[:, 1:2], EPS, None, ALU.add).then_inc(done, 1)

            def start():
                dve.wait_ge(s_wqkv, 48)
                for c in range(DC):
                    for m in range(QCH):
                        nc.vector.tensor_copy(
                            wqkv[:, c, m * P:(m + 1) * P].rearrange("p (d h g) -> p d h g", d=DH, g=GROUPS),
                            wq_raw[:, c].rearrange("p (g m h d) -> p m d h g", g=GROUPS, m=QCH, d=DH)[:, m]
                        ).then_inc(s_wqp, 1)
                nc.vector.memset(ks[ROWS:P], 1.0).then_inc(s_zero, 1)
                nc.vector.memset(ks[0:ROWS, 0, :, 0:WINDOW], 0.0).then_inc(s_zero, 1)
                nc.vector.memset(vals[:, :, :, :, DH:DH + 1], 1.0).then_inc(s_zero, 1)
                nc.vector.memset(vals[:, :, :, :, DH + 1:], 0.0).then_inc(s_zero, 1)
                nc.vector.memset(x2_t[:, 0, :, 0:1], 0.0).then_inc(s_zero, 1)
                for buf in range(2):
                    nc.vector.memset(out_t[:, buf, 0:1], 0.0).then_inc(s_store[buf], 1)
                dve.wait_ge(s_ident, 1)
                nc.vector.tensor_copy(ident_b[:, :], ident[:, :]).then_inc(s_masks, 1)
                for m in range(NCH):
                    hi(0, m)
                    if m:
                        mid_lo(0, m - 1)
                mid_lo(0, NCH - 1)
                val_copy(0, 0)
                dve.wait_ge(s_edge, 16 * 2 * (HPG - 1))
                for n in range(TPB):
                    nc.vector.tensor_copy(edge_mask[:, n], edge_f[:, :, :]).then_inc(s_masks, 1)
                nc.vector.tensor_copy(first_mask[:, :, :], first_f[:, :, :]).then_inc(s_masks, 1)
                tile_q(0, 0, 0, 0)
                tile_q(1, 0, 1, 0)
                for i in range(NMAXB):
                    tile_max(0, i)
                cut_max(0, 0)

            def step(s, j, par, project, maxima, scores):
                t = s * SB_BLKS + j
                f1, f2, f3 = (behind(t, j, scores, n) for n in (1, 2, 3))
                jv, pv = at(j, par, -1)
                u2, u3 = (j - 2) % 2, (j - 3) % 2
                for i in range(NSCORE):
                    if maxima and i < NMAXB // 2:
                        tile_max(t + 1, 2 * i)
                        tile_max(t + 1, 2 * i + 1)
                    if i == 2 and maxima:
                        cut_max(t + 1, j + 1)
                    if i == 1 and f2:
                        dve.wait_ge(s_rstd1, t - 1)
                        if later(t, 4):
                            dve.wait_ge(s_x2tr, t - 3)
                        nc.vector.tensor_scalar(x2[:, u2], y1[:, :], mv1[:, 0:1], rstd1[:, 0:1],
                                                ALU.subtract, ALU.mult).then_inc(s_x2, 1)
                        if later(t, 3):
                            dve.wait_ge(s_x2t, t - 2)
                            nc.vector.tensor_copy(x2_t[:, u2, :, 0:1],
                                                  x2_t[:, 1 - u2, :, BLK:BLK + 1]).then_inc(s_x2p, 1)
                    if i == 1 and f3:
                        dve.wait_ge(s_v, t - 2)
                        dve.wait_ge(s_tanh, t - 2)
                        nc.vector.scalar_tensor_tensor(out=gated[:, :], in0=tanh_r[:, :], scalar=1.0,
                                                       in1=gen0[:, 0:D], op0=ALU.add, op1=ALU.mult).then_inc(s_gated, 1)
                        dve.wait_ge(s_gated, t - 2)
                        nc.vector.scalar_tensor_tensor(out=y2[:, :], in0=gated[:, :], scalar=0.5,
                                                       in1=x2[:, u3], op0=ALU.mult, op1=ALU.add).then_inc(s_y2, 1)
                        moments(t - 3, y2, s_y2, stats2, mv2, var2, s_ln2)
                    if project and j == 1 and i == 0:
                        mid_lo(s + 1, NCH - 1)
                    if project and j == 1 and i == 3:
                        val_copy(s + 1, 1 - par)
                    if i == 3 and f1:
                        dve.wait_ge(s_atr, t)
                        acc = gen1[:, :].rearrange("p (h g v) -> p h g v", h=HPG, v=VCOL)
                        rc = recip[:, :].rearrange("p (h g v) -> p h g v", h=HPG, v=1)
                        nc.vector.reciprocal(rc, acc[:, :, :, DH:DH + 1]).then_inc(s_recip, 1)
                        dve.wait_ge(s_recip, t)
                        if later(t, 2):
                            dve.wait_ge(s_ctr, t - 1)
                        nc.vector.tensor_tensor(att[:, :].rearrange("p (g h v) -> p h g v", g=GROUPS, v=DH),
                                                acc[:, :, :, 0:DH], rc.to_broadcast([P, HPG, GROUPS, DH]),
                                                ALU.mult).then_inc(s_att, 1)
                    if i == 3 and f3:
                        dve.wait_ge(s_rstd2, t - 2)
                        if later(t, 5):
                            dve.wait_ge(s_store[u3], stored(s, j))
                        nc.vector.tensor_scalar(out_t[:, u3], y2[:, :], mv2[:, 0:1], rstd2[:, 0:1],
                                                ALU.subtract, ALU.mult).then_inc(s_out, 1)
                    if i == 4 and f2:
                        dve.wait_ge(s_diff, t - 1)
                        for w in range(2):
                            if later(t, 3):
                                dve.wait_ge(s_k if w else s_r, t - 2)
                            for c in range(DC):
                                nc.vector.scalar_tensor_tensor(
                                    out=mix[:, w, c], in0=diff[:, c], scalar=mu[:, w, c:c + 1],
                                    in1=x2_t[:, u2, c, 0:BLK], op0=ALU.mult, op1=ALU.add).then_inc(s_mix, 1)
                    if project and j == 0 and i >= 5:
                        if i > 5:
                            mid_lo(s + 1, i - 6)
                        hi(s + 1, i - 5)
                    if i == 7 and maxima and (project or j < SB_BLKS - 2):
                        jn, pn = at(j, par, 2)
                        tile_q(t + 2, s if j < SB_BLKS - 2 else s + 1, jn, pn)
                    if i == 7 and f1:
                        dve.wait_ge(s_wo_ps, t)
                        if not later(t, 5):
                            dve.wait_ge(s_xbo, 1)
                        else:
                            dve.wait_ge(s_xbo, s + 1 if j else s)
                        nc.vector.tensor_tensor(y1[:, :], gen1[:, 0:D], x_bo[:, pv, jv], ALU.add).then_inc(s_y1, 1)
                        moments(t - 1, y1, s_y1, stats1, mv1, var1, s_ln1)

            run(dve, start, step)

        @block.tensor
        def _(pe):
            def x_turn(s, c):
                if c == 0:
                    pe.wait_ge(s_x, s * 16 + 16)
                    if later(s, 1):
                        pe.wait_ge(s_val, s)
                else:
                    pe.wait_ge(s_xt, s * DC + 1)
                for b in range(SB_BLKS):
                    ins = nc.tensor.transpose(proj_ps[:, b * BLK:(b + 1) * BLK], x_in[:, b, c * P:(c + 1) * P],
                                              ident[:, :])
                ins.then_inc(s_xtr, 1)

            def project_chunk(s, m):
                if m == 0:
                    pe.wait_ge(s_xt, s * DC + DC)
                else:
                    pe.wait_ge(s_pcp, s * NCH + m)
                for c in range(DC):
                    ins = nc.tensor.matmul(proj_ps[:, 0:SB], wqkv[:, c, m * P:(m + 1) * P], x_t[:, c],
                                           start=(c == 0), stop=(c == DC - 1))
                ins.then_inc(s_proj, 1)

            def v_turn(s):
                pe.wait_ge(s_pcp, s * NCH + NCH)
                for b in range(SB_BLKS):
                    ins = nc.tensor.transpose(proj_ps[:, b * BLK:(b + 1) * BLK],
                                              proj[:, QCH, b * BLK:(b + 1) * BLK], ident[:, :])
                ins.then_inc(s_vtr, 1)

            def max_scores(t, j, par, i):
                if i == 0:
                    pe.wait_ge(s_tiles, t + 1)
                    if later(t, 1):
                        pe.wait_ge(s_maxrow, t)
                elif i >= 2 or later(t, 1):
                    pe.wait_ge(s_max, t * NMAXB + i - 1)
                tiles = range(TPB * i, min(TPB * (i + 1), NTILE))
                out_ps = max_ps[i % 2][:, 0:len(tiles) * TILE_KEYS]
                if later(t, 1):
                    edges = out_ps.rearrange("p (n e k) -> p n e k", n=len(tiles), k=SUB)[:, :, 0::TILE_KEYS // SUB - 1, :]
                    nc.tensor.matmul(edges, ident_b[:, :], edge_mask[:, 0:len(tiles)], start=True, stop=False,
                                     skip_group_check=True)
                for k, tile in enumerate(tiles):
                    g, n = tile // NSUB, tile % NSUB
                    dst = out_ps[:, k * TILE_KEYS:(k + 1) * TILE_KEYS]
                    if not later(t, 1):
                        nc.tensor.matmul(dst, ident_b[:, :], first_mask[:, n], start=(k == 0), stop=False,
                                         skip_group_check=True)
                    k0 = j * BLK + n * SUB
                    ins = nc.tensor.matmul(dst, q_tiles[:, j % 2, tile],
                                           ks[0:ROWS, par, g, k0:k0 + TILE_KEYS], start=False,
                                           stop=(k == len(tiles) - 1), skip_group_check=True)
                ins.then_inc(s_maxsc, 1)

            def max_turn(t, j):
                pe.wait_ge(s_mx, t * 4 + 4)
                pe.nop(nofuse=True)
                nc.tensor.transpose(max_ps[0][0:PARTS * NTILE, 0:P // 2].bitcast(BF16),
                                    max_parts[:, j % 2].rearrange("p a n -> p (a n)"), ident_b[:, :]).then_inc(s_maxtr, 1)

            def score(t, j, par, i):
                g = i // 2
                if i == 0 or (i == 1 and not later(t, 1)):
                    pe.wait_ge(s_maxin, t * MAX_IN + MAX_IN)
                if later(t, 1):
                    pe.wait_ge(s_exp, scored(t, i) - 2)
                elif i > 1:
                    pe.wait_ge(s_exp, scored(t, i) - 1)
                k0 = j * BLK + (WINDOW if i % 2 else 0)
                nc.tensor.matmul(score_ps[i % 2][:, :].rearrange("p (h q) -> p h q", q=BLK),
                                 ks[0:ROWS + PARTS, par, g, k0:k0 + BLK], qs[0:ROWS + PARTS, par, j, :, g, :],
                                 start=True, stop=True).then_inc(s_score, 1)

            def values(t, j, par):
                pe.wait_ge(s_prob, scored(t, NSCORE - 1))
                if later(t, 1):
                    pe.wait_ge(s_att_t, t)
                halves = (0, 1) if later(t, 1) else (1,)
                for half in halves:
                    jk, pk = at(j, par, half - 1)
                    for g in range(GROUPS):
                        ins = nc.tensor.matmul(av_ps[g * VCOL:(g + 1) * VCOL, :], vals[:, pk, jk, g, :],
                                               probs[:, j % 2, 2 * g + half], start=(half == halves[0]),
                                               stop=(half == 1), skip_group_check=True)
                ins.then_inc(s_av, 1)

            def start():
                pe.wait_ge(s_ident, 1)
                x_turn(0, 0)
                x_turn(0, 1)
                pe.wait_ge(s_wqkv, 48)
                pe.wait_ge(s_wqp, DC * QCH)
                for m in range(NCH):
                    project_chunk(0, m)
                v_turn(0)
                pe.wait_ge(s_wffn, 48)
                pe.wait_ge(s_wo, 16)
                for n in range(3):
                    for c in range(DC):
                        if n:
                            pe.wait_ge(s_wcp, DC * (n - 1) + c + 1)
                        for o in range(DC):
                            ins = nc.tensor.transpose((gen0, gen1)[c][:, o * P:(o + 1) * P],
                                                      w_raw[:, n, o, c * P:(c + 1) * P], ident[:, :])
                        ins.then_inc(s_wtr, 1)
                pe.wait_ge(s_zero, 5)
                pe.wait_ge(s_masks, 2 + TPB)
                for i in range(NMAXB):
                    max_scores(0, 0, 0, i)
                max_turn(0, 0)
                pe.wait_ge(s_wcp, 3 * DC)

            def step(s, j, par, project, maxima, scores):
                t = s * SB_BLKS + j
                f1, f2, f3 = (behind(t, j, scores, n) for n in (1, 2, 3))
                jn, pn = at(j, par, 1)
                jv, pv = at(j, par, -1)
                u2 = (j - 2) % 2
                for i in range(NSCORE):
                    if scores and (i % 2 or later(t, 1)):
                        score(t, j, par, i)
                    if maxima and i < NMAXB // 2:
                        max_scores(t + 1, jn, pn, 2 * i)
                        max_scores(t + 1, jn, pn, 2 * i + 1)
                    if i == 0 and f3:
                        pe.wait_ge(s_act_k, t - 2)
                        for c in range(DC):
                            ins = nc.tensor.matmul(gen0[:, 0:D], act_k[:, c], w_t[:, 2, c], start=(c == 0),
                                                   stop=(c == DC - 1))
                        ins.then_inc(s_v, 1)
                    if i == 1 and f1:
                        values(t - 1, jv, pv)
                    if i == 2 and f2:
                        pe.wait_ge(s_x2, t - 1)
                        if f3:
                            pe.wait_ge(s_gated, t - 2)
                        for c in range(DC):
                            ins = nc.tensor.transpose(gen0[:, c * BLK:(c + 1) * BLK], x2[:, u2, c * P:(c + 1) * P],
                                                      ident[:, :])
                        ins.then_inc(s_x2tr, 1)
                    if i == 3 and f1:
                        pe.wait_ge(s_att_t, t)
                        if later(t, 2):
                            pe.wait_ge(s_y1, t - 1)
                        for h in range(HPG):
                            ins = nc.tensor.transpose(gen1[:, h * P:(h + 1) * P], att_t[:, h * BLK:(h + 1) * BLK],
                                                      ident[:, :])
                        ins.then_inc(s_atr, 1)
                    if i == 4 and maxima:
                        max_turn(t + 1, j + 1)
                    if i == 4 and f1:
                        pe.wait_ge(s_att, t)
                        if f2:
                            pe.wait_ge(s_x2t, t - 1)
                        for c in range(DC):
                            ins = nc.tensor.transpose(gen0[:, c * BLK:(c + 1) * BLK], att[:, c * P:(c + 1) * P],
                                                      ident[:, :])
                        ins.then_inc(s_ctr, 1)
                    if i == 5 and f2:
                        pe.wait_ge(s_mix, (t - 2) * 4 + 2)
                        if f1:
                            pe.wait_ge(s_att, t)
                        else:
                            pe.wait_ge(s_y1, t - 1)
                        for c in range(DC):
                            ins = nc.tensor.matmul(gen1[:, 0:D], mix[:, 0, c], w_t[:, 0, c], start=(c == 0),
                                                   stop=(c == DC - 1))
                        ins.then_inc(s_r, 1)
                    if i == 6 and f2:
                        pe.wait_ge(s_mix, (t - 2) * 4 + 4)
                        if f1:
                            pe.wait_ge(s_att_c, t)
                        else:
                            pe.wait_ge(s_x2t, t - 1)
                        for o in range(DC):
                            for c in range(DC):
                                ins = nc.tensor.matmul(gen0[:, o * BLK:(o + 1) * BLK], w_t[:, 1, c, o * P:(o + 1) * P],
                                                       mix[:, 1, c], start=(c == 0), stop=(c == DC - 1))
                        ins.then_inc(s_k, 1)
                    if i == 6 and f1:
                        pe.wait_ge(s_att_c, t)
                        if f2:
                            pe.wait_ge(s_tanh, t - 1)
                        for c in range(DC):
                            ins = nc.tensor.matmul(gen1[:, 0:D], att_c[:, c], wo[:, c], start=(c == 0),
                                                   stop=(c == DC - 1))
                        ins.then_inc(s_wo_ps, 1)
                    if project and j == 0 and i in (2, 3):
                        x_turn(s + 1, i - 2)
                    if project and j == 0 and i in (4, 5, 6):
                        project_chunk(s + 1, i - 4)
                    if project and j == 0 and i == 7:
                        v_turn(s + 1)

            run(pe, start, step)


_INS = ['L0_attn_x', 'L0_attn_Wq', 'L0_attn_bq', 'L0_attn_Wk', 'L0_attn_bk', 'L0_attn_Wv', 'L0_attn_bv', 'L0_attn_Wo',
        'L0_attn_bo', 'L0_ffn_W_r', 'L0_ffn_W_k', 'L0_ffn_W_v', 'L0_ffn_mu_r', 'L0_ffn_mu_k']


def kernel(**inputs):
    import numpy as np
    import concourse.bacc as bacc
    from concourse.bass_utils import run_bass_kernel_spmd

    nc = bacc.Bacc("TRN2", target_bir_lowering=False, num_devices=1)
    arrays, args = {}, []
    for name in _INS:
        a = np.ascontiguousarray(inputs[name])
        arrays[f"in_{name}"] = a
        args.append(nc.dram_tensor(f"in_{name}", a.shape, mybir.dt.from_np(a.dtype), kind="ExternalInput").ap())
    shape = inputs['L0_attn_x'].shape
    args.append(nc.dram_tensor("out_0", shape, F32, kind="ExternalOutput").ap())
    attention_channel_mix(nc, *args)
    r = run_bass_kernel_spmd(nc, [arrays], core_ids=[0])
    return r.results[0]["out_0"]
```

```python
from contextlib import ExitStack

import concourse.bass as bass
from concourse import mybir

F32 = mybir.dt.float32
BF16 = mybir.dt.bfloat16
ALU = mybir.AluOpType
ACT = mybir.ActivationFunctionType
AX_X = mybir.AxisListType.X

P = 128
HEADS = 16
GROUPS = 4
HPG = HEADS // GROUPS
WINDOW = 128
BLK = 128
SUB = 32
NSUB = BLK // SUB
TILE_KEYS = WINDOW + SUB
SB_BLKS = 4
SB = SB_BLKS * BLK
NTILE = GROUPS * NSUB
TPB = 3
NMAXB = -(-NTILE // TPB)
NSCORE = 2 * GROUPS
PARTS = 3
Q_PART = (0, 0, 0, 1, 1, 2)
K_PART = (0, 1, 2, 0, 1, 0)
NREP = len(Q_PART)
VCOL = 32
MASKED = -1e30
EPS = 1e-5


def attention_channel_mix(nc, x, Wq, bq, Wk, bk, Wv, bv, Wo, bo, W_r, W_k, W_v, mu_r, mu_k, out):
    S, D = x.shape[1], x.shape[2]
    DH = D // HEADS
    DKV = GROUPS * DH
    DC = D // P
    NBLK = S // BLK
    NSB = S // SB
    QCH = D // P
    NCH = QCH + 1
    ROWS = NREP * DH
    SCALE = float(DH) ** -0.5
    assert 2 * DKV == P and ROWS == 96 and NBLK % SB_BLKS == 0 and NSB % 2 == 0

    BIAS_COL = (NCH + 2 * DC - 1,) + tuple(range(QCH))
    MU_COL = QCH
    assert QCH * 2 == HPG and GROUPS * SUB == BLK
    x_sb = x.rearrange("b (s j p) d -> (b s) p j d", j=SB_BLKS, p=BLK)
    out_blk = out.rearrange("b (t p) d -> (b t) p d", p=BLK)

    q_dram = nc.dram_tensor("q_parts", [2, PARTS, SB_BLKS, QCH, P, BLK], BF16, kind="Internal").ap()
    k_dram = nc.dram_tensor("k_parts", [PARTS, DKV, S], BF16, kind="Internal").ap()

    SPILLS = 16 * PARTS * QCH
    STACKS = 16 * 2 * NREP
    MAX_IN = 16 * HPG
    N_CONST = 8
    N_SMALL = 16 * 6
    N_COLS = NCH + 2 * DC

    with ExitStack() as ctx:
        def sb(name, shape, dt=F32):
            return ctx.enter_context(nc.sbuf_tensor(name, shape, dt))

        def bank(name, dt=F32):
            return ctx.enter_context(nc.psum_tensor(name, [P, 512], dt))

        def sem(name):
            return ctx.enter_context(nc.semaphore(name))

        ident = sb("ident", [P, P])
        ident_b = sb("ident_b", [P, P], BF16)
        edge_f = sb("edge_f", [P, 2, SUB])
        edge_mask = sb("edge_mask", [P, TPB, 2, SUB], BF16)
        first_f = sb("first_f", [P, NSUB, TILE_KEYS])
        first_mask = sb("first_mask", [P, NSUB, TILE_KEYS], BF16)
        wq_raw = sb("wq_raw", [P, DC, D])
        wqkv = sb("wqkv", [P, DC, 2 * DKV + D])
        wo = sb("wo", [P, DC, D])
        w_raw = sb("w_raw", [P, 3, DC, D])
        w_t = sb("w_t", [P, 3, DC, D])
        bq_rows = sb("bq_rows", [QCH, P])
        small_rows = sb("small_rows", [NCH + 2 * DC, P])
        small_cols = sb("small_cols", [P, NCH + 2 * DC])
        bo_b = sb("bo_b", [P, D])
        minus_half = sb("minus_half", [P, 1])
        warm = sb("warm", [P, 1])
        x_in = sb("x_in", [P, SB_BLKS, D])
        x_bo = sb("x_bo", [P, 2, SB_BLKS, D])
        x_t = sb("x_t", [P, DC, SB])
        proj = sb("proj", [P, NCH, SB])
        rest = sb("rest", [P, NCH, SB])
        parts = sb("parts", [P, NCH, PARTS, SB], BF16)
        qs = sb("qs", [P, 2, SB_BLKS, HPG, GROUPS, BLK], BF16)
        ks = sb("ks", [P, 2, GROUPS, WINDOW + SB], BF16)
        vals = sb("vals", [P, 2, SB_BLKS, GROUPS, VCOL])
        q_tiles = sb("q_tiles", [ROWS, 2, NTILE, HPG * SUB], BF16)
        neg_max = sb("neg_max", [P, NTILE])
        max_rest = sb("max_rest", [P, NTILE])
        max_parts = sb("max_parts", [P, 2, PARTS, NTILE], BF16)
        max_rows = sb("max_rows", [P, 2, P], BF16)
        probs = sb("probs", [P, 2, NSCORE, HPG * BLK])
        att_t = sb("att_t", [P, HPG * BLK])
        recip = sb("recip", [P, HEADS])
        att = sb("att", [P, D])
        att_c = sb("att_c", [P, DC, BLK])
        y1 = sb("y1", [P, D])
        stats1 = sb("stats1", [P, 6])
        mv1 = sb("mv1", [P, 2])
        var1 = sb("var1", [P, 1])
        rstd1 = sb("rstd1", [P, 1])
        x2 = sb("x2", [P, 2, D])
        x2_t = sb("x2_t", [P, 2, DC, 1 + BLK])
        diff = sb("diff", [P, DC, BLK])
        mix = sb("mix", [P, 2, DC, BLK])
        tanh_r = sb("tanh_r", [P, D])
        relu_k = sb("relu_k", [P, DC, BLK])
        act_k = sb("act_k", [P, DC, BLK])
        gated = sb("gated", [P, D])
        y2 = sb("y2", [P, D])
        stats2 = sb("stats2", [P, 6])
        mv2 = sb("mv2", [P, 2])
        var2 = sb("var2", [P, 1])
        rstd2 = sb("rstd2", [P, 1])
        out_t = sb("out_t", [P, 2, D])

        max_ps = [bank(f"max_ps{i}") for i in range(2)]
        score_ps = [bank(f"score_ps{i}") for i in range(2)]
        av_ps = bank("av_ps")
        gen0 = bank("gen0")
        gen1 = bank("gen1")
        proj_ps = bank("proj_ps")

        s_ident = sem("s_ident")
        s_const = sem("s_const")
        s_edge = sem("s_edge")
        s_masks = sem("s_masks")
        s_zero = sem("s_zero")
        s_wkv = sem("s_wkv")
        s_wq = sem("s_wq")
        s_bqp = sem("s_bqp")
        s_smalltr = sem("s_smalltr")
        s_cols = sem("s_cols")
        s_wo = sem("s_wo")
        s_wffn = sem("s_wffn")
        s_small = sem("s_small")
        s_wtr = sem("s_wtr")
        s_wcp = sem("s_wcp")
        s_x = sem("s_x")
        s_xbo = sem("s_xbo")
        s_xtr = sem("s_xtr")
        s_xt = sem("s_xt")
        s_proj = sem("s_proj")
        s_pcp = sem("s_pcp")
        s_vtr = sem("s_vtr")
        s_val = sem("s_val")
        s_hi = sem("s_hi")
        s_rest = sem("s_rest")
        s_mid = sem("s_mid")
        s_lo = sem("s_lo")
        s_spill_k = sem("s_spill_k")
        s_spill_q = sem("s_spill_q")
        s_stack = sem("s_stack")
        s_tiles = sem("s_tiles")
        s_maxsc = sem("s_maxsc")
        s_max = sem("s_max")
        s_mx = sem("s_mx")
        s_maxtr = sem("s_maxtr")
        s_maxrow = sem("s_maxrow")
        s_maxin = sem("s_maxin")
        s_score = sem("s_score")
        s_exp = sem("s_exp")
        s_prob = sem("s_prob")
        s_av = sem("s_av")
        s_att_t = sem("s_att_t")
        s_atr = sem("s_atr")
        s_recip = sem("s_recip")
        s_att = sem("s_att")
        s_ctr = sem("s_ctr")
        s_att_c = sem("s_att_c")
        s_wo_ps = sem("s_wo_ps")
        s_y1 = sem("s_y1")
        s_ln1 = sem("s_ln1")
        s_rstd1 = sem("s_rstd1")
        s_x2 = sem("s_x2")
        s_x2tr = sem("s_x2tr")
        s_x2t = sem("s_x2t")
        s_x2p = sem("s_x2p")
        s_diff = sem("s_diff")
        s_mix = sem("s_mix")
        s_r = sem("s_r")
        s_k = sem("s_k")
        s_tanh = sem("s_tanh")
        s_relu = sem("s_relu")
        s_act_k = sem("s_act_k")
        s_v = sem("s_v")
        s_gated = sem("s_gated")
        s_y2 = sem("s_y2")
        s_ln2 = sem("s_ln2")
        s_rstd2 = sem("s_rstd2")
        s_wqp = sem("s_wqp")
        s_out = sem("s_out")
        s_store = [sem("s_store0"), sem("s_store1")]

        def later(t, n):
            return not isinstance(t, int) or t >= n

        def at(j, par, d):
            return (j + d) % SB_BLKS, par ^ ((j + d) // SB_BLKS & 1)

        def stored(s, j):
            return s * (16 * SB_BLKS // 2) + 16 * ((j - 5) // 2 + 1) + 1

        def scored(t, i):
            if isinstance(t, int) and t == 0:
                return i // 2 + 1
            return t * NSCORE - NSCORE // 2 + i + 1

        block = ctx.enter_context(nc.Block())

        def run(eng, start, step, tail=None):
            def superblock(s, par, last=False):
                for j in range(SB_BLKS):
                    step(s, j, par, project=not last, maxima=not last or j < SB_BLKS - 1, scores=True)

            start()
            superblock(0, 0)
            with eng.Fori(0, (NSB - 2) // 2) as pair:
                superblock(pair * 2 + 1, 1)
                superblock(pair * 2 + 2, 0)
            superblock(NSB - 1, 1, last=True)
            for j in range(SB_BLKS, SB_BLKS + 3):
                step(NSB - 1, j, 1, project=False, maxima=False, scores=False)
            if tail:
                tail()

        def behind(t, j, scores, n):
            return later(t, n) and (scores or j - n < SB_BLKS)

        @block.sync
        def _(sp):
            def load_x(s):
                sp.dma_start(x_in[:, :, :], x_sb[s]).then_inc(s_x, 16)

            def spill_q(s, par, m):
                sp.wait_ge(s_lo, s * NCH + m + 2)
                sp.nop(nofuse=True)
                for a in range(PARTS):
                    sp.dma_start(q_dram[par, a, :, m].rearrange("j p t -> p j t"),
                                 parts[:, 1 + m, a, :].rearrange("p (j t) -> p j t", t=BLK)).then_inc(s_spill_q, 16)

            def spill_k(s):
                sp.wait_ge(s_lo, s * NCH + 1)
                sp.nop(nofuse=True)
                sp.dma_start(k_dram[:, :, bass.ds(s * SB, SB)].rearrange("a p t -> p a t"),
                             parts[0:DKV, 0]).then_inc(s_spill_k, 16)

            def stack_q(s, par, rep):
                if rep == 0:
                    sp.wait_ge(s_spill_q, s * SPILLS + SPILLS)
                    sp.nop(nofuse=True)
                    if later(s, 2):
                        sp.wait_ge(s_score, scored(s * SB_BLKS - SB_BLKS - 1, NSCORE - 1))
                        sp.nop(nofuse=True)
                sp.dma_start(qs[rep * DH:(rep + 1) * DH, par].rearrange("d j (m x) g t -> d (j m) (x g t)", m=QCH),
                             q_dram[par, Q_PART[rep]].rearrange("j m (d y) t -> d (j m) (y t)", d=DH)
                             ).then_inc(s_stack, 16)

            def stack_k(s, par, rep):
                if rep == 0:
                    sp.wait_ge(s_spill_k, s * 16 + 16)
                    sp.nop(nofuse=True)
                src = k_dram[K_PART[rep]].rearrange("(g d) t -> d g t", d=DH)
                if not later(s, 1):
                    sp.dma_start(ks[rep * DH:(rep + 1) * DH, par, :, WINDOW:], src[:, :, 0:SB]).then_inc(s_stack, 16)
                else:
                    sp.dma_start(ks[rep * DH:(rep + 1) * DH, par],
                                 src[:, :, bass.ds(s * SB - WINDOW, WINDOW + SB)]).then_inc(s_stack, 16)

            def max_in(t, j, par):
                sp.wait_ge(s_maxrow, t + 1)
                sp.nop(nofuse=True)
                for h in range(HPG):
                    sp.dma_start(qs[ROWS:ROWS + PARTS, par, j, h].rearrange("a g t -> a (g t)"),
                                 max_rows[0:PARTS * NTILE, j % 2, h * SUB:(h + 1) * SUB]).then_inc(s_maxin, 16)

            def store(t, buf):
                sp.wait_ge(s_out, t + 1)
                sp.nop(nofuse=True)
                sp.dma_start(out_blk[t], out_t[:, buf]).then_inc(s_store[buf], 16)

            def start():
                load_x(0)
                sp.dma_start(wqkv[:, :, 0:DKV], Wk.rearrange("(c p) n -> p c n", p=P)).then_inc(s_wkv, 16)
                sp.dma_start(wqkv[:, :, DKV:2 * DKV], Wv.rearrange("(c p) n -> p c n", p=P)).then_inc(s_wkv, 16)
                sp.dma_start(wq_raw[:, :, :], Wq.rearrange("(c p) n -> p c n", p=P)).then_inc(s_wq, 16)
                for n, w in enumerate((W_r, W_k, W_v)):
                    sp.dma_start(w_raw[:, n], w.rearrange("(c p) n -> p c n", p=P)).then_inc(s_wffn, 16)
                sp.wait_ge(s_const, N_CONST)
                sp.nop(nofuse=True)
                for h in range(1, HPG):
                    sp.dma_start(edge_f[h * SUB:(h + 1) * SUB], edge_f[0:SUB]).then_inc(s_edge, 16)
                    sp.dma_start(first_f[h * SUB:(h + 1) * SUB], first_f[0:SUB]).then_inc(s_edge, 16)
                sp.dma_start(wo[:, :, :], Wo.rearrange("(c p) n -> p c n", p=P)).then_inc(s_wo, 16)
                spill_k(0)
                for m in range(QCH):
                    spill_q(0, 0, m)
                for rep in range(NREP):
                    stack_k(0, 0, rep)
                for rep in range(NREP):
                    stack_q(0, 0, rep)
                max_in(0, 0, 0)

            def step(s, j, par, project, maxima, scores):
                t = s * SB_BLKS + j
                def x_ahead():
                    sp.wait_ge(s_xtr, s * DC + DC)
                    sp.nop(nofuse=True)
                    sp.wait_ge(s_xbo, s + 1)
                    sp.nop(nofuse=True)
                    load_x(s + 1)

                if project and j == 2:
                    stack_k(s + 1, 1 - par, 3)
                    stack_k(s + 1, 1 - par, 4)
                    stack_k(s + 1, 1 - par, 5)
                if project and j == 1:
                    stack_k(s + 1, 1 - par, 0)
                    stack_k(s + 1, 1 - par, 1)
                    stack_k(s + 1, 1 - par, 2)
                if project and j == 2:
                    stack_q(s + 1, 1 - par, 0)
                    stack_q(s + 1, 1 - par, 1)
                    stack_q(s + 1, 1 - par, 2)
                if project and j == 0:
                    x_ahead()
                if project and j == 2:
                    stack_q(s + 1, 1 - par, 3)
                    stack_q(s + 1, 1 - par, 4)
                    stack_q(s + 1, 1 - par, 5)
                if maxima:
                    max_in(t + 1, *at(j, par, 1))
                if project and j == 0:
                    spill_q(s + 1, 1 - par, 0)
                    spill_k(s + 1)
                    spill_q(s + 1, 1 - par, 1)
                if behind(t, j, scores, 3):
                    store(t - 3, (j - 3) % 2)

            def tail():
                for buf in range(2):
                    sp.wait_ge(s_store[buf], 16 * (NBLK // 2) + 1)
                    sp.nop(nofuse=True)

            run(sp, start, step, tail)

        @block.gpsimd
        def _(pool):
            def x_plus_bo(s, par):
                pool.wait_ge(s_x, s * 16 + 16)
                nc.gpsimd.tensor_tensor(x_bo[:, par], x_in[:, :, :],
                                        bo_b[:, :].unsqueeze(1).to_broadcast([P, SB_BLKS, D]), ALU.add).then_inc(s_xbo, 1)

            def rest_of(s, m):
                pool.wait_ge(s_hi, s * NCH + m + 1)
                nc.gpsimd.tensor_tensor(rest[:, m], proj[:, m], parts[:, m, 0], ALU.subtract).then_inc(s_rest, 1)

            def mask(t, i, buf):
                pool.wait_ge(s_exp, scored(t, i))
                pool.nop(nofuse=True)
                v = probs[:, buf, i].rearrange("p (h q) -> p h q", q=BLK)
                sign = 1 if i % 2 else -1
                nc.gpsimd.affine_select(out=v, in_=v, compare_op=ALU.is_ge if i % 2 else ALU.is_gt, fill=0.0,
                                        base=0, pattern=[[0, HPG], [sign, BLK]],
                                        channel_multiplier=-sign).then_inc(s_prob, 1)

            def rstd(u, var, out_, ready, steps, done):
                pool.wait_ge(ready, u * steps + steps)
                nc.gpsimd.tensor_tensor(out_[:, :], var[:, :], minus_half[:, :], ALU.pow).then_inc(done, 1)

            def start():
                nc.gpsimd.memset(ident[:, :], 0.0).then_inc(s_const, 1)
                nc.gpsimd.memset(edge_f[0:SUB], 0.0).then_inc(s_const, 1)
                nc.gpsimd.memset(first_f[0:SUB], 0.0).then_inc(s_const, 1)
                nc.gpsimd.memset(minus_half[:, :], -0.5).then_inc(s_const, 1)
                pool.wait_ge(s_const, 4)
                nc.gpsimd.affine_select(out=ident[:, :], in_=ident[:, :], compare_op=ALU.not_equal, fill=1.0, base=0,
                                        pattern=[[-1, P]], channel_multiplier=1).then_inc(s_ident, 1)
                nc.gpsimd.affine_select(out=edge_f[0:SUB, 0], in_=edge_f[0:SUB, 0], compare_op=ALU.is_gt, fill=MASKED,
                                        base=0, pattern=[[1, SUB]], channel_multiplier=-1).then_inc(s_const, 1)
                nc.gpsimd.affine_select(out=edge_f[0:SUB, 1], in_=edge_f[0:SUB, 1], compare_op=ALU.is_ge, fill=MASKED,
                                        base=0, pattern=[[-1, SUB]], channel_multiplier=1).then_inc(s_const, 1)
                nc.gpsimd.affine_select(out=first_f[0:SUB], in_=first_f[0:SUB], compare_op=ALU.is_ge, fill=MASKED,
                                        base=-WINDOW, pattern=[[SUB, NSUB], [1, TILE_KEYS]],
                                        channel_multiplier=0).then_inc(s_const, 1)
                pool.wait_ge(s_const, 7)
                nc.gpsimd.affine_select(out=first_f[0:SUB, :, WINDOW:], in_=first_f[0:SUB, :, WINDOW:],
                                        compare_op=ALU.is_ge, fill=MASKED, base=0, pattern=[[0, NSUB], [-1, SUB]],
                                        channel_multiplier=1).then_inc(s_const, 1)
                nc.gpsimd.memset(ks[ROWS:P], 1.0).then_inc(s_const, 1)
                pool.wait_ge(s_const, N_CONST + 1)
                for m in range(NCH):
                    rest_of(0, m)
                pool.wait_ge(s_small, N_SMALL)
                x_plus_bo(0, 0)

            def step(s, j, par, project, maxima, scores):
                t = s * SB_BLKS + j
                f1, f2, f3 = (behind(t, j, scores, n) for n in (1, 2, 3))
                jn, pn = at(j, par, 1)
                jv, pv = at(j, par, -1)
                u2, u3 = (j - 2) % 2, (j - 3) % 2
                def difference():
                    pool.wait_ge(s_x2t, t - 1)
                    if later(t, 3):
                        pool.wait_ge(s_x2p, t - 2)
                    nc.gpsimd.tensor_tensor(diff[:, :, :], x2_t[:, u2, :, 1:], x2_t[:, u2, :, 0:BLK],
                                            ALU.subtract).then_inc(s_diff, 1)

                def square():
                    pool.wait_ge(s_relu, t - 1)
                    nc.gpsimd.tensor_tensor(act_k[:, :, :], relu_k[:, :, :], relu_k[:, :, :],
                                            ALU.mult).then_inc(s_act_k, 1)

                def add_bo():
                    if later(s, 1):
                        pool.wait_ge(s_y1, s * SB_BLKS)
                    x_plus_bo(s + 1, 1 - par)

                if f2:
                    rstd(t - 2, var1, rstd1, s_ln1, 3, s_rstd1)
                if scores and later(t, 1):
                    mask(t, 0, j % 2)
                if scores:
                    mask(t, 1, j % 2)
                if project and j == 2:
                    add_bo()
                if f2:
                    difference()
                if f3:
                    rstd(t - 3, var2, rstd2, s_ln2, 3, s_rstd2)
                if scores and later(t, 1):
                    mask(t, 2, j % 2)
                if scores:
                    mask(t, 3, j % 2)
                if project and j == 0:
                    rest_of(s + 1, 0)
                if scores and later(t, 1):
                    mask(t, 4, j % 2)
                if project and j == 0:
                    rest_of(s + 1, 1)
                if scores and later(t, 1):
                    mask(t, 6, j % 2)
                if scores:
                    mask(t, 7, j % 2)
                if project and j == 0:
                    rest_of(s + 1, 2)
                if f2:
                    square()
                if scores:
                    mask(t, 5, j % 2)

            run(pool, start, step)

        @block.scalar
        def _(act):
            def x_t_copy(s, c, ps=None):
                act.wait_ge(s_xtr, s * DC + c + 1)
                if later(s, 1):
                    act.wait_ge(s_proj, s * NCH)
                nc.scalar.copy(x_t[:, c], (ps or proj_ps)[:, 0:SB]).then_inc(s_xt, 1)

            def proj_copy(s, m, ps=None):
                act.wait_ge(s_proj, s * NCH + m + 1)
                if later(s, 1):
                    act.wait_ge(s_lo, s * NCH - NCH + m + 1)
                    if m == 0:
                        act.wait_ge(s_vtr, s)
                nc.scalar.activation(proj[:, m], (ps or proj_ps)[:, 0:SB], ACT.Identity,
                                     bias=small_cols[:, BIAS_COL[m]:BIAS_COL[m] + 1]).then_inc(s_pcp, 1)

            def max_row_copy(t, j):
                act.wait_ge(s_maxtr, t + 1)
                if later(t, 2):
                    act.wait_ge(s_maxin, t * MAX_IN - MAX_IN)
                nc.scalar.copy(max_rows[0:PARTS * NTILE, j % 2],
                               max_ps[0][0:PARTS * NTILE, 0:P // 2].bitcast(BF16)).then_inc(s_maxrow, 1)

            def exps(t, i, buf):
                act.wait_ge(s_score, scored(t, i))
                if i <= 1 and later(t, 2):
                    act.wait_ge(s_av, t - 1)
                nc.scalar.activation(probs[:, buf, i], score_ps[i % 2][:, :], ACT.Exp, scale=SCALE).then_inc(s_exp, 1)

            def start():
                act.dma_start(bq_rows[:, :].rearrange("m (g r) -> m g r", g=GROUPS),
                              bq.rearrange("(g m r) -> m g r", g=GROUPS, m=QCH)).then_inc(s_small, 16)
                act.dma_start(small_rows[QCH:QCH + DC], mu_r.rearrange("(c p) -> c p", p=P)).then_inc(s_small, 16)
                act.dma_start(small_rows[QCH + DC:QCH + 2 * DC], mu_k.rearrange("(c p) -> c p", p=P)).then_inc(s_small, 16)
                act.dma_start(small_rows[N_COLS - 1:N_COLS, 0:DKV], bk.rearrange("(o n) -> o n", o=1)).then_inc(s_small, 16)
                act.dma_start(small_rows[N_COLS - 1:N_COLS, DKV:P], bv.rearrange("(o n) -> o n", o=1)).then_inc(s_small, 16)
                act.dma_start(bo_b[:, :], bo.rearrange("(o n) -> o n", o=1).to_broadcast([P, D])).then_inc(s_small, 16)
                act.wait_ge(s_const, 4)
                nc.scalar.activation(warm[:, :], minus_half[:, :], ACT.Exp)
                for c in range(DC):
                    x_t_copy(0, c, (gen0, gen1)[c])
                act.wait_ge(s_cols, 1)
                for m in range(NCH):
                    proj_copy(0, m, (proj_ps, max_ps[0], max_ps[1])[m])
                for n in range(3):
                    for c in range(DC):
                        act.wait_ge(s_wtr, DC * n + c + 1)
                        nc.scalar.copy(w_t[:, n, c], (gen0, gen1)[c][:, 0:D]).then_inc(s_wcp, 1)
                max_row_copy(0, 0)

            def step(s, j, par, project, maxima, scores):
                t = s * SB_BLKS + j
                f1, f2, f3 = (behind(t, j, scores, n) for n in (1, 2, 3))
                jn, pn = at(j, par, 1)
                jv, pv = at(j, par, -1)
                u2, u3 = (j - 2) % 2, (j - 3) % 2
                def att_t_copy():
                    act.wait_ge(s_av, t)
                    nc.scalar.copy(att_t[:, :], av_ps[:, :]).then_inc(s_att_t, 1)

                def x2_t_copy():
                    act.wait_ge(s_x2tr, t - 1)
                    if later(t, 4):
                        act.wait_ge(s_mix, (t - 3) * 4)
                    nc.scalar.copy(x2_t[:, (j - 2) % 2, :, 1:],
                                   gen0[:, 0:DC * BLK].rearrange("p (c q) -> p c q", q=BLK)).then_inc(s_x2t, 1)

                def att_c_copy():
                    act.wait_ge(s_ctr, t)
                    nc.scalar.copy(att_c[:, :, :],
                                   gen0[:, 0:D].rearrange("p (c q) -> p c q", q=BLK)).then_inc(s_att_c, 1)

                def tanh():
                    act.wait_ge(s_r, t - 1)
                    nc.scalar.activation(tanh_r[:, :], gen1[:, 0:D], ACT.Tanh, scale=0.5).then_inc(s_tanh, 1)

                def relu():
                    act.wait_ge(s_k, t - 1)
                    nc.scalar.activation(relu_k[:, :, :], gen0[:, 0:DC * BLK].rearrange("p (c q) -> p c q", q=BLK),
                                         ACT.Relu).then_inc(s_relu, 1)

                if scores and later(t, 1):
                    exps(t, 0, j % 2)
                if project and j == 0:
                    x_t_copy(s + 1, 0)
                if scores:
                    exps(t, 1, j % 2)
                if scores and later(t, 1):
                    exps(t, 2, j % 2)
                if f1:
                    att_t_copy()
                if f2:
                    x2_t_copy()
                if project and j == 0:
                    x_t_copy(s + 1, 1)
                if scores:
                    exps(t, 3, j % 2)
                if maxima:
                    max_row_copy(t + 1, j + 1)
                if scores and later(t, 1):
                    exps(t, 4, j % 2)
                if project and j == 0:
                    proj_copy(s + 1, 0)
                if f1:
                    att_c_copy()
                if scores:
                    exps(t, 5, j % 2)
                if f2:
                    tanh()
                if project and j == 0:
                    proj_copy(s + 1, 1)
                if scores and later(t, 1):
                    exps(t, 6, j % 2)
                if project and j == 0:
                    proj_copy(s + 1, 2)
                if scores:
                    exps(t, 7, j % 2)
                if f2:
                    relu()

            run(act, start, step)

        @block.vector
        def _(dve):
            def hi(s, m):
                dve.wait_ge(s_pcp, s * NCH + m + 1)
                if later(s, 1):
                    if m:
                        dve.wait_ge(s_spill_q, s * SPILLS)
                    else:
                        dve.wait_ge(s_spill_k, s * 16)
                nc.vector.tensor_copy(parts[:, m, 0], proj[:, m]).then_inc(s_hi, 1)

            def mid_lo(s, m):
                dve.wait_ge(s_rest, s * NCH + m + 1)
                nc.vector.tensor_copy(parts[:, m, 1], rest[:, m]).then_inc(s_mid, 1)
                dve.wait_ge(s_mid, s * NCH + m + 1)
                nc.vector.tensor_tensor(parts[:, m, 2], rest[:, m], parts[:, m, 1], ALU.subtract).then_inc(s_lo, 1)

            def val_copy(s, par):
                dve.wait_ge(s_vtr, s + 1)
                if later(s, 2):
                    dve.wait_ge(s_av, s * SB_BLKS - 3)
                nc.vector.tensor_copy(vals[:, par, :, :, 0:DH],
                                      proj_ps[:, 0:SB].rearrange("p (j x g d) -> p j x g d", x=2, g=GROUPS, d=DH)[:, :, 1]
                                      ).then_inc(s_val, 1)

            def tile_q(t, s, j, par):
                if j == 0:
                    dve.wait_ge(s_stack, s * STACKS + STACKS)
                nc.vector.tensor_copy(q_tiles[:, j % 2].rearrange("r n (h q) -> r n h q", q=SUB),
                                      qs[0:ROWS, par, j].rearrange("r h g (n q) -> r (g n) h q", q=SUB)
                                      ).then_inc(s_tiles, 1)

            def tile_max(t, i):
                n = min(TPB, NTILE - TPB * i)
                dve.wait_ge(s_maxsc, t * NMAXB + i + 1)
                nc.vector.tensor_reduce(neg_max[:, TPB * i:TPB * i + n],
                                        max_ps[i % 2][:, 0:n * TILE_KEYS].rearrange("p (n k) -> p n k", k=TILE_KEYS),
                                        AX_X, ALU.max, negate=True).then_inc(s_max, 1)

            def cut_max(t, j):
                mp = max_parts[:, j % 2]
                dve.wait_ge(s_max, t * NMAXB + NMAXB)
                nc.vector.tensor_copy(mp[:, 0], neg_max[:, :]).then_inc(s_mx, 1)
                dve.wait_ge(s_mx, t * 4 + 1)
                nc.vector.tensor_tensor(max_rest[:, :], neg_max[:, :], mp[:, 0], ALU.subtract).then_inc(s_mx, 1)
                dve.wait_ge(s_mx, t * 4 + 2)
                nc.vector.tensor_copy(mp[:, 1], max_rest[:, :]).then_inc(s_mx, 1)
                dve.wait_ge(s_mx, t * 4 + 3)
                nc.vector.tensor_tensor(mp[:, 2], max_rest[:, :], mp[:, 1], ALU.subtract).then_inc(s_mx, 1)

            def moments(u, y, y_done, stats, mv, var, done):
                dve.wait_ge(y_done, u + 1)
                nc.vector.bn_stats(stats[:, :], y[:, :]).then_inc(done, 1)
                dve.wait_ge(done, u * 3 + 1)
                dve.nop(nofuse=True)
                nc.vector.bn_aggr(mv[:, :], stats[:, :]).then_inc(done, 1)
                dve.wait_ge(done, u * 3 + 2)
                nc.vector.tensor_scalar(var[:, :], mv[:, 1:2], EPS, None, ALU.add).then_inc(done, 1)

            def start():
                dve.wait_ge(s_small, N_SMALL)
                nc.vector.tensor_copy(small_rows[0:QCH].rearrange("m (d h g) -> m d h g", d=DH, g=GROUPS),
                                      bq_rows[:, :].rearrange("m (g h d) -> m d h g", g=GROUPS, d=DH)).then_inc(s_bqp, 1)
                dve.wait_ge(s_wq, 16)
                for c in range(DC):
                    for m in range(QCH):
                        nc.vector.tensor_copy(
                            wqkv[:, c, (1 + m) * P:(2 + m) * P].rearrange("p (d h g) -> p d h g", d=DH, g=GROUPS),
                            wq_raw[:, c].rearrange("p (g m h d) -> p m d h g", g=GROUPS, m=QCH, d=DH)[:, m]
                        ).then_inc(s_wqp, 1)
                dve.wait_ge(s_smalltr, 1)
                nc.vector.tensor_copy(small_cols[:, :], score_ps[0][:, 0:N_COLS]).then_inc(s_cols, 1)
                dve.wait_ge(s_cols, 1)
                nc.vector.memset(ks[0:ROWS, 0, :, 0:WINDOW], 0.0).then_inc(s_zero, 1)
                nc.vector.memset(vals[:, :, :, :, DH:DH + 1], 1.0).then_inc(s_zero, 1)
                nc.vector.memset(vals[:, :, :, :, DH + 1:], 0.0).then_inc(s_zero, 1)
                nc.vector.memset(x2_t[:, 0, :, 0:1], 0.0).then_inc(s_zero, 1)
                for buf in range(2):
                    nc.vector.memset(out_t[:, buf, 0:1], 0.0).then_inc(s_store[buf], 1)
                dve.wait_ge(s_ident, 1)
                nc.vector.tensor_copy(ident_b[:, :], ident[:, :]).then_inc(s_masks, 1)
                for m in range(NCH):
                    hi(0, m)
                    if m:
                        mid_lo(0, m - 1)
                mid_lo(0, NCH - 1)
                val_copy(0, 0)
                dve.wait_ge(s_edge, 16 * 2 * (HPG - 1))
                for n in range(TPB):
                    nc.vector.tensor_copy(edge_mask[:, n], edge_f[:, :, :]).then_inc(s_masks, 1)
                nc.vector.tensor_copy(first_mask[:, :, :], first_f[:, :, :]).then_inc(s_masks, 1)
                tile_q(0, 0, 0, 0)
                tile_q(1, 0, 1, 0)
                for i in range(NMAXB):
                    tile_max(0, i)
                cut_max(0, 0)

            def step(s, j, par, project, maxima, scores):
                t = s * SB_BLKS + j
                f1, f2, f3 = (behind(t, j, scores, n) for n in (1, 2, 3))
                jn, pn = at(j, par, 1)
                jv, pv = at(j, par, -1)
                u2, u3 = (j - 2) % 2, (j - 3) % 2
                def first_norm():
                    dve.wait_ge(s_rstd1, t - 1)
                    if later(t, 4):
                        dve.wait_ge(s_x2tr, t - 3)
                    nc.vector.tensor_scalar(x2[:, u2], y1[:, :], mv1[:, 0:1], rstd1[:, 0:1],
                                            ALU.subtract, ALU.mult).then_inc(s_x2, 1)

                def token_before():
                    if later(t, 3):
                        dve.wait_ge(s_x2t, t - 2)
                        nc.vector.tensor_copy(x2_t[:, u2, :, 0:1],
                                              x2_t[:, 1 - u2, :, BLK:BLK + 1]).then_inc(s_x2p, 1)

                def gate():
                    dve.wait_ge(s_v, t - 2)
                    dve.wait_ge(s_tanh, t - 2)
                    nc.vector.scalar_tensor_tensor(out=gated[:, :], in0=tanh_r[:, :], scalar=1.0,
                                                   in1=gen0[:, 0:D], op0=ALU.add, op1=ALU.mult).then_inc(s_gated, 1)

                def second_residual():
                    dve.wait_ge(s_gated, t - 2)
                    nc.vector.scalar_tensor_tensor(out=y2[:, :], in0=gated[:, :], scalar=0.5,
                                                   in1=x2[:, u3], op0=ALU.mult, op1=ALU.add).then_inc(s_y2, 1)
                    moments(t - 3, y2, s_y2, stats2, mv2, var2, s_ln2)

                def normalise():
                    dve.wait_ge(s_atr, t)
                    acc = gen1[:, :].rearrange("p (h g v) -> p h g v", h=HPG, v=VCOL)
                    rc = recip[:, :].rearrange("p (h g v) -> p h g v", h=HPG, v=1)
                    nc.vector.reciprocal(rc, acc[:, :, :, DH:DH + 1]).then_inc(s_recip, 1)
                    dve.wait_ge(s_recip, t)
                    if later(t, 2):
                        dve.wait_ge(s_ctr, t - 1)
                    nc.vector.tensor_tensor(att[:, :].rearrange("p (g h v) -> p h g v", g=GROUPS, v=DH),
                                            acc[:, :, :, 0:DH], rc.to_broadcast([P, HPG, GROUPS, DH]),
                                            ALU.mult).then_inc(s_att, 1)

                def second_norm():
                    dve.wait_ge(s_rstd2, t - 2)
                    if later(t, 5):
                        dve.wait_ge(s_store[u3], stored(s, j))
                    nc.vector.tensor_scalar(out_t[:, u3], y2[:, :], mv2[:, 0:1], rstd2[:, 0:1],
                                            ALU.subtract, ALU.mult).then_inc(s_out, 1)

                def mixes():
                    dve.wait_ge(s_diff, t - 1)
                    for w in range(2):
                        if later(t, 3):
                            dve.wait_ge(s_k if w else s_r, t - 2)
                        for c in range(DC):
                            nc.vector.scalar_tensor_tensor(
                                out=mix[:, w, c], in0=diff[:, c], scalar=small_cols[:, MU_COL + w * DC + c:MU_COL + w * DC + c + 1],
                                in1=x2_t[:, u2, c, 0:BLK], op0=ALU.mult, op1=ALU.add).then_inc(s_mix, 1)

                def tiles_ahead():
                    jn, pn = at(j, par, 2)
                    tile_q(t + 2, s if j < SB_BLKS - 2 else s + 1, jn, pn)

                def first_residual():
                    dve.wait_ge(s_wo_ps, t)
                    if not later(t, 5):
                        dve.wait_ge(s_xbo, 1)
                    else:
                        dve.wait_ge(s_xbo, s + 1 if j else s)
                    nc.vector.tensor_tensor(y1[:, :], gen1[:, 0:D], x_bo[:, pv, jv], ALU.add).then_inc(s_y1, 1)
                    moments(t - 1, y1, s_y1, stats1, mv1, var1, s_ln1)

                if maxima:
                    tile_max(t + 1, 0)
                if f2:
                    token_before()
                if maxima:
                    tile_max(t + 1, 1)
                if project and j == 1:
                    mid_lo(s + 1, 2)
                if f2:
                    first_norm()
                if maxima:
                    tile_max(t + 1, 2)
                    tile_max(t + 1, 3)
                if f3:
                    gate()
                    second_residual()
                if maxima:
                    tile_max(t + 1, 4)
                    tile_max(t + 1, 5)
                    cut_max(t + 1, j + 1)
                if f1:
                    normalise()
                if f2:
                    mixes()
                if maxima and (project or j < SB_BLKS - 2):
                    tiles_ahead()
                if project and j == 0:
                    hi(s + 1, 0)
                    hi(s + 1, 1)
                if project and j == 1:
                    val_copy(s + 1, 1 - par)
                if f3:
                    second_norm()
                if project and j == 0:
                    mid_lo(s + 1, 0)
                    mid_lo(s + 1, 1)
                    hi(s + 1, 2)
                if f1:
                    first_residual()

            run(dve, start, step)

        @block.tensor
        def _(pe):
            def x_turn(s, c, ps=None):
                if c == 0:
                    pe.wait_ge(s_x, s * 16 + 16)
                    if later(s, 1):
                        pe.wait_ge(s_val, s)
                elif ps is None:
                    pe.wait_ge(s_xt, s * DC + 1)
                for b in range(SB_BLKS):
                    ins = nc.tensor.transpose((ps or proj_ps)[:, b * BLK:(b + 1) * BLK], x_in[:, b, c * P:(c + 1) * P],
                                              ident[:, :])
                ins.then_inc(s_xtr, 1)

            def project_chunk(s, m, ps=None):
                if m == 0:
                    pe.wait_ge(s_xt, s * DC + DC)
                elif ps is None:
                    pe.wait_ge(s_pcp, s * NCH + m)
                for c in range(DC):
                    ins = nc.tensor.matmul((ps or proj_ps)[:, 0:SB], wqkv[:, c, m * P:(m + 1) * P], x_t[:, c],
                                           start=(c == 0), stop=(c == DC - 1))
                ins.then_inc(s_proj, 1)

            def v_turn(s):
                pe.wait_ge(s_pcp, s * NCH + NCH)
                for b in range(SB_BLKS):
                    ins = nc.tensor.transpose(proj_ps[:, b * BLK:(b + 1) * BLK],
                                              proj[:, 0, b * BLK:(b + 1) * BLK], ident[:, :])
                ins.then_inc(s_vtr, 1)

            def max_scores(t, j, par, i):
                if i == 0:
                    pe.wait_ge(s_tiles, t + 1)
                    if later(t, 1):
                        pe.wait_ge(s_maxrow, t)
                elif i >= 2 or later(t, 1):
                    pe.wait_ge(s_max, t * NMAXB + i - 1)
                tiles = range(TPB * i, min(TPB * (i + 1), NTILE))
                out_ps = max_ps[i % 2][:, 0:len(tiles) * TILE_KEYS]
                if later(t, 1):
                    edges = out_ps.rearrange("p (n e k) -> p n e k", n=len(tiles), k=SUB)[:, :, 0::TILE_KEYS // SUB - 1, :]
                    nc.tensor.matmul(edges, ident_b[:, :], edge_mask[:, 0:len(tiles)], start=True, stop=False,
                                     skip_group_check=True)
                for k, tile in enumerate(tiles):
                    g, n = tile // NSUB, tile % NSUB
                    dst = out_ps[:, k * TILE_KEYS:(k + 1) * TILE_KEYS]
                    if not later(t, 1):
                        nc.tensor.matmul(dst, ident_b[:, :], first_mask[:, n], start=(k == 0), stop=False,
                                         skip_group_check=True)
                    k0 = j * BLK + n * SUB
                    ins = nc.tensor.matmul(dst, q_tiles[:, j % 2, tile],
                                           ks[0:ROWS, par, g, k0:k0 + TILE_KEYS], start=False,
                                           stop=(k == len(tiles) - 1), skip_group_check=True)
                ins.then_inc(s_maxsc, 1)

            def max_turn(t, j):
                pe.wait_ge(s_mx, t * 4 + 4)
                pe.nop(nofuse=True)
                nc.tensor.transpose(max_ps[0][0:PARTS * NTILE, 0:P // 2].bitcast(BF16),
                                    max_parts[:, j % 2].rearrange("p a n -> p (a n)"), ident_b[:, :]).then_inc(s_maxtr, 1)

            def score(t, j, par, i):
                g = i // 2
                if i == 0 or (i == 1 and not later(t, 1)):
                    pe.wait_ge(s_maxin, t * MAX_IN + MAX_IN)
                if later(t, 1):
                    pe.wait_ge(s_exp, scored(t, i) - 2)
                elif i > 1:
                    pe.wait_ge(s_exp, scored(t, i) - 1)
                k0 = j * BLK + (WINDOW if i % 2 else 0)
                nc.tensor.matmul(score_ps[i % 2][:, :].rearrange("p (h q) -> p h q", q=BLK),
                                 ks[0:ROWS + PARTS, par, g, k0:k0 + BLK], qs[0:ROWS + PARTS, par, j, :, g, :],
                                 start=True, stop=True).then_inc(s_score, 1)

            def values(t, j, par):
                pe.wait_ge(s_prob, scored(t, NSCORE - 1))
                if later(t, 1):
                    pe.wait_ge(s_att_t, t)
                halves = (0, 1) if later(t, 1) else (1,)
                for half in halves:
                    jk, pk = at(j, par, half - 1)
                    for g in range(GROUPS):
                        ins = nc.tensor.matmul(av_ps[g * VCOL:(g + 1) * VCOL, :], vals[:, pk, jk, g, :],
                                               probs[:, j % 2, 2 * g + half], start=(half == halves[0]),
                                               stop=(half == 1), skip_group_check=True)
                ins.then_inc(s_av, 1)

            def start():
                pe.wait_ge(s_ident, 1)
                for c in range(DC):
                    x_turn(0, c, (gen0, gen1)[c])
                pe.wait_ge(s_small, N_SMALL)
                pe.wait_ge(s_bqp, 1)
                nc.tensor.transpose(score_ps[0][:, 0:N_COLS], small_rows[:, :], ident[0:N_COLS, 0:N_COLS]).then_inc(s_smalltr, 1)
                pe.wait_ge(s_wkv, 32)
                for m in range(NCH):
                    if m == 1:
                        pe.wait_ge(s_wqp, DC * QCH)
                    project_chunk(0, m, (proj_ps, max_ps[0], max_ps[1])[m])
                v_turn(0)
                pe.wait_ge(s_wffn, 48)
                pe.wait_ge(s_wo, 16)
                for n in range(3):
                    for c in range(DC):
                        if n:
                            pe.wait_ge(s_wcp, DC * (n - 1) + c + 1)
                        for o in range(DC):
                            ins = nc.tensor.transpose((gen0, gen1)[c][:, o * P:(o + 1) * P],
                                                      w_raw[:, n, o, c * P:(c + 1) * P], ident[:, :])
                        ins.then_inc(s_wtr, 1)
                pe.wait_ge(s_zero, 4)
                pe.wait_ge(s_const, N_CONST + 1)
                pe.wait_ge(s_masks, 2 + TPB)
                for i in range(NMAXB):
                    max_scores(0, 0, 0, i)
                max_turn(0, 0)
                pe.wait_ge(s_wcp, 3 * DC)

            def step(s, j, par, project, maxima, scores):
                t = s * SB_BLKS + j
                f1, f2, f3 = (behind(t, j, scores, n) for n in (1, 2, 3))
                jn, pn = at(j, par, 1)
                jv, pv = at(j, par, -1)
                u2, u3 = (j - 2) % 2, (j - 3) % 2
                def second_product():
                    pe.wait_ge(s_act_k, t - 2)
                    for c in range(DC):
                        ins = nc.tensor.matmul(gen0[:, 0:D], act_k[:, c], w_t[:, 2, c], start=(c == 0),
                                               stop=(c == DC - 1))
                    ins.then_inc(s_v, 1)

                def turn_x2():
                    pe.wait_ge(s_x2, t - 1)
                    if f3:
                        pe.wait_ge(s_gated, t - 2)
                    for c in range(DC):
                        ins = nc.tensor.transpose(gen0[:, c * BLK:(c + 1) * BLK], x2[:, u2, c * P:(c + 1) * P],
                                                  ident[:, :])
                    ins.then_inc(s_x2tr, 1)

                def turn_back():
                    pe.wait_ge(s_att_t, t)
                    if later(t, 2):
                        pe.wait_ge(s_y1, t - 1)
                    for h in range(HPG):
                        ins = nc.tensor.transpose(gen1[:, h * P:(h + 1) * P], att_t[:, h * BLK:(h + 1) * BLK],
                                                  ident[:, :])
                    ins.then_inc(s_atr, 1)

                def turn_attention():
                    pe.wait_ge(s_att, t)
                    if f2:
                        pe.wait_ge(s_x2t, t - 1)
                    for c in range(DC):
                        ins = nc.tensor.transpose(gen0[:, c * BLK:(c + 1) * BLK], att[:, c * P:(c + 1) * P],
                                                  ident[:, :])
                    ins.then_inc(s_ctr, 1)

                def r_product():
                    pe.wait_ge(s_mix, (t - 2) * 4 + 2)
                    if f1:
                        pe.wait_ge(s_att, t)
                    else:
                        pe.wait_ge(s_y1, t - 1)
                    for c in range(DC):
                        ins = nc.tensor.matmul(gen1[:, 0:D], mix[:, 0, c], w_t[:, 0, c], start=(c == 0),
                                               stop=(c == DC - 1))
                    ins.then_inc(s_r, 1)

                def k_product():
                    pe.wait_ge(s_mix, (t - 2) * 4 + 4)
                    if f1:
                        pe.wait_ge(s_att_c, t)
                    else:
                        pe.wait_ge(s_x2t, t - 1)
                    for o in range(DC):
                        for c in range(DC):
                            ins = nc.tensor.matmul(gen0[:, o * BLK:(o + 1) * BLK], w_t[:, 1, c, o * P:(o + 1) * P],
                                                   mix[:, 1, c], start=(c == 0), stop=(c == DC - 1))
                    ins.then_inc(s_k, 1)

                def output_product():
                    pe.wait_ge(s_att_c, t)
                    if f2:
                        pe.wait_ge(s_tanh, t - 1)
                    for c in range(DC):
                        ins = nc.tensor.matmul(gen1[:, 0:D], att_c[:, c], wo[:, c], start=(c == 0),
                                               stop=(c == DC - 1))
                    ins.then_inc(s_wo_ps, 1)

                if maxima:
                    max_scores(t + 1, jn, pn, 0)
                    max_scores(t + 1, jn, pn, 1)
                if scores and later(t, 1):
                    score(t, j, par, 0)
                if maxima:
                    max_scores(t + 1, jn, pn, 2)
                if f3:
                    second_product()
                if scores:
                    score(t, j, par, 1)
                if maxima:
                    max_scores(t + 1, jn, pn, 3)
                if project and j == 0:
                    x_turn(s + 1, 0)
                if f1:
                    values(t - 1, jv, pv)
                if scores and later(t, 1):
                    score(t, j, par, 2)
                if maxima:
                    max_scores(t + 1, jn, pn, 4)
                    max_scores(t + 1, jn, pn, 5)
                if f2:
                    turn_x2()
                if scores:
                    score(t, j, par, 3)
                if project and j == 0:
                    x_turn(s + 1, 1)
                if project and j == 1:
                    v_turn(s + 1)
                if f1:
                    turn_back()
                if maxima:
                    max_turn(t + 1, j + 1)
                if scores and later(t, 1):
                    score(t, j, par, 4)
                if project and j == 0:
                    project_chunk(s + 1, 0)
                if f1:
                    turn_attention()
                if scores:
                    score(t, j, par, 5)
                if f2:
                    r_product()
                if project and j == 0:
                    project_chunk(s + 1, 1)
                if scores and later(t, 1):
                    score(t, j, par, 6)
                if project and j == 0:
                    project_chunk(s + 1, 2)
                if scores:
                    score(t, j, par, 7)
                if f1:
                    output_product()
                if f2:
                    k_product()

            run(pe, start, step)


_INS = ['L0_attn_x', 'L0_attn_Wq', 'L0_attn_bq', 'L0_attn_Wk', 'L0_attn_bk', 'L0_attn_Wv', 'L0_attn_bv', 'L0_attn_Wo',
        'L0_attn_bo', 'L0_ffn_W_r', 'L0_ffn_W_k', 'L0_ffn_W_v', 'L0_ffn_mu_r', 'L0_ffn_mu_k']


def kernel(**inputs):
    import numpy as np
    import concourse.bacc as bacc
    from concourse.bass_utils import run_bass_kernel_spmd

    nc = bacc.Bacc("TRN2", target_bir_lowering=False, num_devices=1)
    arrays, args = {}, []
    for name in _INS:
        a = np.ascontiguousarray(inputs[name])
        arrays[f"in_{name}"] = a
        args.append(nc.dram_tensor(f"in_{name}", a.shape, mybir.dt.from_np(a.dtype), kind="ExternalInput").ap())
    shape = inputs['L0_attn_x'].shape
    args.append(nc.dram_tensor("out_0", shape, F32, kind="ExternalOutput").ap())
    attention_channel_mix(nc, *args)
    r = run_bass_kernel_spmd(nc, [arrays], core_ids=[0])
    return r.results[0]["out_0"]
```

```python
from contextlib import ExitStack

import concourse.bass as bass
from concourse import mybir

F32 = mybir.dt.float32
BF16 = mybir.dt.bfloat16
ALU = mybir.AluOpType
ACT = mybir.ActivationFunctionType
AX_X = mybir.AxisListType.X

P = 128
HEADS = 16
GROUPS = 4
HPG = HEADS // GROUPS
WINDOW = 128
BLK = 128
SUB = 32
NSUB = BLK // SUB
TILE_KEYS = WINDOW + SUB
SB_BLKS = 4
SB = SB_BLKS * BLK
NTILE = GROUPS * NSUB
TPB = 3
NMAXB = -(-NTILE // TPB)
NSCORE = 2 * GROUPS
PARTS = 3
Q_PART = (0, 0, 0, 1, 1, 2)
K_PART = (0, 1, 2, 0, 1, 0)
NREP = len(Q_PART)
VCOL = 32
MASKED = -1e30
THREE_BANKS = (1, 2, 3)
EPS = 1e-5


def attention_channel_mix(nc, x, Wq, bq, Wk, bk, Wv, bv, Wo, bo, W_r, W_k, W_v, mu_r, mu_k, out):
    S, D = x.shape[1], x.shape[2]
    DH = D // HEADS
    DKV = GROUPS * DH
    DC = D // P
    NBLK = S // BLK
    NSB = S // SB
    QCH = D // P
    NCH = QCH + 1
    ROWS = NREP * DH
    SCALE = float(DH) ** -0.5
    assert 2 * DKV == P and ROWS == 96 and NBLK % SB_BLKS == 0 and NSB % 2 == 0

    BIAS_COL = (NCH + 2 * DC - 1,) + tuple(range(QCH))
    MU_COL = QCH
    assert QCH * 2 == HPG and GROUPS * SUB == BLK
    x_sb = x.rearrange("b (s j p) d -> (b s) p j d", j=SB_BLKS, p=BLK)
    out_blk = out.rearrange("b (t p) d -> (b t) p d", p=BLK)

    q_dram = nc.dram_tensor("q_parts", [2, PARTS, SB_BLKS, QCH, P, BLK], BF16, kind="Internal").ap()
    k_dram = nc.dram_tensor("k_parts", [PARTS, DKV, S], BF16, kind="Internal").ap()

    SPILLS = 16 * PARTS * QCH
    STACKS = 16 * 2 * NREP
    MAX_IN = 16 * HPG
    N_CONST = 8
    N_SMALL = 16 * 6
    N_COLS = NCH + 2 * DC

    with ExitStack() as ctx:
        def sb(name, shape, dt=F32):
            return ctx.enter_context(nc.sbuf_tensor(name, shape, dt))

        def bank(name, dt=F32):
            return ctx.enter_context(nc.psum_tensor(name, [P, 512], dt))

        def sem(name):
            return ctx.enter_context(nc.semaphore(name))

        ident = sb("ident", [P, P])
        ident_b = sb("ident_b", [P, P], BF16)
        edge_f = sb("edge_f", [P, 2, SUB])
        edge_mask = sb("edge_mask", [P, TPB, 2, SUB], BF16)
        first_f = sb("first_f", [P, NSUB, TILE_KEYS])
        first_mask = sb("first_mask", [P, NSUB, TILE_KEYS], BF16)
        wq_raw = sb("wq_raw", [P, DC, D])
        wqkv = sb("wqkv", [P, DC, 2 * DKV + D])
        wo = sb("wo", [P, DC, D])
        w_raw = sb("w_raw", [P, 3, DC, D])
        w_t = sb("w_t", [P, 3, DC, D])
        bq_rows = sb("bq_rows", [QCH, P])
        small_rows = sb("small_rows", [NCH + 2 * DC, P])
        small_cols = sb("small_cols", [P, NCH + 2 * DC])
        bo_b = sb("bo_b", [P, D])
        minus_half = sb("minus_half", [P, 1])
        warm = sb("warm", [P, 1])
        x_in = sb("x_in", [P, SB_BLKS, D])
        x_bo = sb("x_bo", [P, 2, SB_BLKS, D])
        x_t = sb("x_t", [P, DC, SB])
        proj = sb("proj", [P, NCH, SB])
        rest = sb("rest", [P, NCH, SB])
        parts = sb("parts", [P, NCH, PARTS, SB], BF16)
        qs = sb("qs", [P, 2, SB_BLKS, HPG, GROUPS, BLK], BF16)
        ks = sb("ks", [P, 2, GROUPS, WINDOW + SB], BF16)
        vals = sb("vals", [P, 2, SB_BLKS, GROUPS, VCOL])
        q_tiles = sb("q_tiles", [ROWS, 2, NTILE, HPG * SUB], BF16)
        neg_max = sb("neg_max", [P, NTILE])
        max_rest = sb("max_rest", [P, NTILE])
        max_parts = sb("max_parts", [P, 2, PARTS, NTILE], BF16)
        max_rows = sb("max_rows", [P, 2, P], BF16)
        probs = sb("probs", [P, 2, NSCORE, HPG * BLK])
        att_t = sb("att_t", [P, HPG * BLK])
        recip = sb("recip", [P, HEADS])
        att = sb("att", [P, D])
        att_c = sb("att_c", [P, DC, BLK])
        y1 = sb("y1", [P, D])
        stats1 = sb("stats1", [P, 6])
        mv1 = sb("mv1", [P, 2])
        var1 = sb("var1", [P, 1])
        rstd1 = sb("rstd1", [P, 1])
        x2 = sb("x2", [P, 2, D])
        x2_t = sb("x2_t", [P, 2, DC, 1 + BLK])
        diff = sb("diff", [P, DC, BLK])
        mix = sb("mix", [P, 2, DC, BLK])
        tanh_r = sb("tanh_r", [P, D])
        relu_k = sb("relu_k", [P, DC, BLK])
        act_k = sb("act_k", [P, DC, BLK])
        gated = sb("gated", [P, D])
        y2 = sb("y2", [P, D])
        stats2 = sb("stats2", [P, 6])
        mv2 = sb("mv2", [P, 2])
        var2 = sb("var2", [P, 1])
        rstd2 = sb("rstd2", [P, 1])
        out_t = sb("out_t", [P, 2, D])

        max_ps = [bank(f"max_ps{i}") for i in range(2)]
        score_ps = [bank(f"score_ps{i}") for i in range(2)]
        av_ps = bank("av_ps")
        gen0 = bank("gen0")
        gen1 = bank("gen1")
        proj_ps = bank("proj_ps")

        s_ident = sem("s_ident")
        s_const = sem("s_const")
        s_edge = sem("s_edge")
        s_masks = sem("s_masks")
        s_zero = sem("s_zero")
        s_wkv = sem("s_wkv")
        s_wq = sem("s_wq")
        s_bqp = sem("s_bqp")
        s_smalltr = sem("s_smalltr")
        s_cols = sem("s_cols")
        s_wo = sem("s_wo")
        s_wffn = sem("s_wffn")
        s_small = sem("s_small")
        s_wtr = sem("s_wtr")
        s_wcp = sem("s_wcp")
        s_x = sem("s_x")
        s_xbo = sem("s_xbo")
        s_xtr = sem("s_xtr")
        s_xt = sem("s_xt")
        s_proj = sem("s_proj")
        s_pcp = sem("s_pcp")
        s_vtr = sem("s_vtr")
        s_val = sem("s_val")
        s_hi = sem("s_hi")
        s_rest = sem("s_rest")
        s_mid = sem("s_mid")
        s_lo = sem("s_lo")
        s_spill_k = sem("s_spill_k")
        s_spill_q = sem("s_spill_q")
        s_stack = sem("s_stack")
        s_tiles = sem("s_tiles")
        s_maxsc = sem("s_maxsc")
        s_max = sem("s_max")
        s_mx = sem("s_mx")
        s_maxtr = sem("s_maxtr")
        s_maxrow = sem("s_maxrow")
        s_maxin = sem("s_maxin")
        s_score = sem("s_score")
        s_exp = sem("s_exp")
        s_prob = sem("s_prob")
        s_av = sem("s_av")
        s_att_t = sem("s_att_t")
        s_atr = sem("s_atr")
        s_recip = sem("s_recip")
        s_att = sem("s_att")
        s_ctr = sem("s_ctr")
        s_att_c = sem("s_att_c")
        s_wo_ps = sem("s_wo_ps")
        s_y1 = sem("s_y1")
        s_ln1 = sem("s_ln1")
        s_rstd1 = sem("s_rstd1")
        s_x2 = sem("s_x2")
        s_x2tr = sem("s_x2tr")
        s_x2t = sem("s_x2t")
        s_x2p = sem("s_x2p")
        s_diff = sem("s_diff")
        s_mix = sem("s_mix")
        s_r = sem("s_r")
        s_k = sem("s_k")
        s_tanh = sem("s_tanh")
        s_relu = sem("s_relu")
        s_act_k = sem("s_act_k")
        s_v = sem("s_v")
        s_gated = sem("s_gated")
        s_y2 = sem("s_y2")
        s_ln2 = sem("s_ln2")
        s_rstd2 = sem("s_rstd2")
        s_wqp = sem("s_wqp")
        s_out = sem("s_out")
        s_store = [sem("s_store0"), sem("s_store1")]

        def later(t, n):
            return not isinstance(t, int) or t >= n

        def at(j, par, d):
            return (j + d) % SB_BLKS, par ^ ((j + d) // SB_BLKS & 1)

        def stored(s, j):
            return s * (16 * SB_BLKS // 2) + 16 * ((j - 5) // 2 + 1) + 1

        def scored(t, i):
            if isinstance(t, int) and t == 0:
                return i // 2 + 1
            return t * NSCORE - NSCORE // 2 + i + 1

        def max_bank(t, j, i):
            if j in THREE_BANKS and later(t, 1):
                return (max_ps[0], max_ps[1], proj_ps)[i % 3]
            return max_ps[i % 2]

        block = ctx.enter_context(nc.Block())

        def run(eng, start, step, tail=None):
            def superblock(s, par, left=2):
                for j in range(SB_BLKS):
                    step(s, j, par, project=left > 0, coming=left > 1, maxima=left > 0 or j < SB_BLKS - 1,
                         scores=True)

            start()
            superblock(0, 0)
            with eng.Fori(0, (NSB - 4) // 2) as pair:
                superblock(pair * 2 + 1, 1)
                superblock(pair * 2 + 2, 0)
            for left in (2, 1, 0):
                superblock(NSB - 1 - left, (NSB - 1 - left) % 2, left)
            for j in range(SB_BLKS, SB_BLKS + 3):
                step(NSB - 1, j, 1, project=False, coming=False, maxima=False, scores=False)
            if tail:
                tail()

        def behind(t, j, scores, n):
            return later(t, n) and (scores or j - n < SB_BLKS)

        @block.sync
        def _(sp):
            def load_x(s):
                if later(s, 1):
                    sp.wait_ge(s_xtr, s * DC)
                    sp.nop(nofuse=True)
                    sp.wait_ge(s_xbo, s)
                    sp.nop(nofuse=True)
                sp.dma_start(x_in[:, :, :], x_sb[s]).then_inc(s_x, 16)

            def spill_q(s, par, m):
                sp.wait_ge(s_lo, s * NCH + m + 2)
                sp.nop(nofuse=True)
                for a in range(PARTS):
                    sp.dma_start(q_dram[par, a, :, m].rearrange("j p t -> p j t"),
                                 parts[:, 1 + m, a, :].rearrange("p (j t) -> p j t", t=BLK)).then_inc(s_spill_q, 16)

            def spill_k(s):
                sp.wait_ge(s_lo, s * NCH + 1)
                sp.nop(nofuse=True)
                sp.dma_start(k_dram[:, :, bass.ds(s * SB, SB)].rearrange("a p t -> p a t"),
                             parts[0:DKV, 0]).then_inc(s_spill_k, 16)

            def stack_q(s, par, rep):
                if rep == 0:
                    sp.wait_ge(s_spill_q, s * SPILLS + SPILLS)
                    sp.nop(nofuse=True)
                    if later(s, 2):
                        sp.wait_ge(s_score, scored(s * SB_BLKS - SB_BLKS - 1, NSCORE - 1))
                        sp.nop(nofuse=True)
                sp.dma_start(qs[rep * DH:(rep + 1) * DH, par].rearrange("d j (m x) g t -> d (j m) (x g t)", m=QCH),
                             q_dram[par, Q_PART[rep]].rearrange("j m (d y) t -> d (j m) (y t)", d=DH)
                             ).then_inc(s_stack, 16)

            def stack_k(s, par, rep):
                if rep == 0:
                    sp.wait_ge(s_spill_k, s * 16 + 16)
                    sp.nop(nofuse=True)
                src = k_dram[K_PART[rep]].rearrange("(g d) t -> d g t", d=DH)
                if not later(s, 1):
                    sp.dma_start(ks[rep * DH:(rep + 1) * DH, par, :, WINDOW:], src[:, :, 0:SB]).then_inc(s_stack, 16)
                else:
                    sp.dma_start(ks[rep * DH:(rep + 1) * DH, par],
                                 src[:, :, bass.ds(s * SB - WINDOW, WINDOW + SB)]).then_inc(s_stack, 16)

            def max_in(t, j, par):
                sp.wait_ge(s_maxrow, t + 1)
                sp.nop(nofuse=True)
                for h in range(HPG):
                    sp.dma_start(qs[ROWS:ROWS + PARTS, par, j, h].rearrange("a g t -> a (g t)"),
                                 max_rows[0:PARTS * NTILE, j % 2, h * SUB:(h + 1) * SUB]).then_inc(s_maxin, 16)

            def store(t, buf):
                sp.wait_ge(s_out, t + 1)
                sp.nop(nofuse=True)
                sp.dma_start(out_blk[t], out_t[:, buf]).then_inc(s_store[buf], 16)

            def start():
                load_x(0)
                sp.dma_start(wqkv[:, :, 0:DKV], Wk.rearrange("(c p) n -> p c n", p=P)).then_inc(s_wkv, 16)
                sp.dma_start(wqkv[:, :, DKV:2 * DKV], Wv.rearrange("(c p) n -> p c n", p=P)).then_inc(s_wkv, 16)
                sp.dma_start(wq_raw[:, :, :], Wq.rearrange("(c p) n -> p c n", p=P)).then_inc(s_wq, 16)
                for n, w in enumerate((W_r, W_k, W_v)):
                    sp.dma_start(w_raw[:, n], w.rearrange("(c p) n -> p c n", p=P)).then_inc(s_wffn, 16)
                sp.wait_ge(s_const, N_CONST)
                sp.nop(nofuse=True)
                for h in range(1, HPG):
                    sp.dma_start(edge_f[h * SUB:(h + 1) * SUB], edge_f[0:SUB]).then_inc(s_edge, 16)
                    sp.dma_start(first_f[h * SUB:(h + 1) * SUB], first_f[0:SUB]).then_inc(s_edge, 16)
                sp.dma_start(wo[:, :, :], Wo.rearrange("(c p) n -> p c n", p=P)).then_inc(s_wo, 16)
                load_x(1)
                spill_k(0)
                for m in range(QCH):
                    spill_q(0, 0, m)
                for rep in range(NREP):
                    stack_k(0, 0, rep)
                for rep in range(NREP):
                    stack_q(0, 0, rep)
                max_in(0, 0, 0)

            def step(s, j, par, project, coming, maxima, scores):
                t = s * SB_BLKS + j

                if project and j == 2:
                    for rep in range(3, NREP):
                        stack_k(s + 1, 1 - par, rep)
                    for rep in range(3, NREP):
                        stack_q(s + 1, 1 - par, rep)
                if project and j == 0:
                    spill_k(s + 1)
                if coming and j == 2:
                    load_x(s + 2)
                if project and j == 1:
                    spill_q(s + 1, 1 - par, 1)
                if maxima:
                    max_in(t + 1, *at(j, par, 1))
                if project and j == 0:
                    spill_q(s + 1, 1 - par, 0)
                    for rep in range(3):
                        stack_k(s + 1, 1 - par, rep)
                if project and j == 1:
                    for rep in range(3):
                        stack_q(s + 1, 1 - par, rep)
                if behind(t, j, scores, 3):
                    store(t - 3, (j - 3) % 2)

            def tail():
                for buf in range(2):
                    sp.wait_ge(s_store[buf], 16 * (NBLK // 2) + 1)
                    sp.nop(nofuse=True)

            run(sp, start, step, tail)

        @block.gpsimd
        def _(pool):
            def x_plus_bo(s, par):
                if later(s, 2):
                    pool.wait_ge(s_y1, (s - 1) * SB_BLKS)
                pool.wait_ge(s_x, s * 16 + 16)
                nc.gpsimd.tensor_tensor(x_bo[:, par], x_in[:, :, :],
                                        bo_b[:, :].unsqueeze(1).to_broadcast([P, SB_BLKS, D]), ALU.add).then_inc(s_xbo, 1)

            def rest_of(s, m):
                pool.wait_ge(s_hi, s * NCH + m + 1)
                nc.gpsimd.tensor_tensor(rest[:, m], proj[:, m], parts[:, m, 0], ALU.subtract).then_inc(s_rest, 1)

            def mask(t, i, buf):
                pool.wait_ge(s_exp, scored(t, i))
                pool.nop(nofuse=True)
                v = probs[:, buf, i].rearrange("p (h q) -> p h q", q=BLK)
                sign = 1 if i % 2 else -1
                nc.gpsimd.affine_select(out=v, in_=v, compare_op=ALU.is_ge if i % 2 else ALU.is_gt, fill=0.0,
                                        base=0, pattern=[[0, HPG], [sign, BLK]],
                                        channel_multiplier=-sign).then_inc(s_prob, 1)

            def rstd(u, var, out_, ready, steps, done):
                pool.wait_ge(ready, u * steps + steps)
                nc.gpsimd.tensor_tensor(out_[:, :], var[:, :], minus_half[:, :], ALU.pow).then_inc(done, 1)

            def start():
                nc.gpsimd.memset(ident[:, :], 0.0).then_inc(s_const, 1)
                nc.gpsimd.memset(edge_f[0:SUB], 0.0).then_inc(s_const, 1)
                nc.gpsimd.memset(first_f[0:SUB], 0.0).then_inc(s_const, 1)
                nc.gpsimd.memset(minus_half[:, :], -0.5).then_inc(s_const, 1)
                pool.wait_ge(s_const, 4)
                nc.gpsimd.affine_select(out=ident[:, :], in_=ident[:, :], compare_op=ALU.not_equal, fill=1.0, base=0,
                                        pattern=[[-1, P]], channel_multiplier=1).then_inc(s_ident, 1)
                nc.gpsimd.affine_select(out=edge_f[0:SUB, 0], in_=edge_f[0:SUB, 0], compare_op=ALU.is_gt, fill=MASKED,
                                        base=0, pattern=[[1, SUB]], channel_multiplier=-1).then_inc(s_const, 1)
                nc.gpsimd.affine_select(out=edge_f[0:SUB, 1], in_=edge_f[0:SUB, 1], compare_op=ALU.is_ge, fill=MASKED,
                                        base=0, pattern=[[-1, SUB]], channel_multiplier=1).then_inc(s_const, 1)
                nc.gpsimd.affine_select(out=first_f[0:SUB], in_=first_f[0:SUB], compare_op=ALU.is_ge, fill=MASKED,
                                        base=-WINDOW, pattern=[[SUB, NSUB], [1, TILE_KEYS]],
                                        channel_multiplier=0).then_inc(s_const, 1)
                pool.wait_ge(s_const, 7)
                nc.gpsimd.affine_select(out=first_f[0:SUB, :, WINDOW:], in_=first_f[0:SUB, :, WINDOW:],
                                        compare_op=ALU.is_ge, fill=MASKED, base=0, pattern=[[0, NSUB], [-1, SUB]],
                                        channel_multiplier=1).then_inc(s_const, 1)
                nc.gpsimd.memset(ks[ROWS:P], 1.0).then_inc(s_const, 1)
                pool.wait_ge(s_const, N_CONST + 1)
                pool.wait_ge(s_small, N_SMALL)
                x_plus_bo(0, 0)
                for m in range(NCH):
                    rest_of(0, m)
                x_plus_bo(1, 1)
                for m in range(NCH):
                    rest_of(1, m)

            def step(s, j, par, project, coming, maxima, scores):
                t = s * SB_BLKS + j
                ahead = project and later(s, 1)
                f2, f3 = (behind(t, j, scores, n) for n in (2, 3))
                u2 = (j - 2) % 2

                def difference():
                    pool.wait_ge(s_x2t, t - 1)
                    if later(t, 3):
                        pool.wait_ge(s_x2p, t - 2)
                    nc.gpsimd.tensor_tensor(diff[:, :, :], x2_t[:, u2, :, 1:], x2_t[:, u2, :, 0:BLK],
                                            ALU.subtract).then_inc(s_diff, 1)

                if f2:
                    rstd(t - 2, var1, rstd1, s_ln1, 3, s_rstd1)
                if ahead and j == 2:
                    x_plus_bo(s + 1, 1 - par)
                if scores:
                    mask(t, 1, j % 2)
                if scores and later(t, 1):
                    mask(t, 2, j % 2)
                if f2:
                    difference()
                if f3:
                    rstd(t - 3, var2, rstd2, s_ln2, 3, s_rstd2)
                if scores and later(t, 1):
                    mask(t, 0, j % 2)
                if coming and j == 3:
                    rest_of(s + 2, 0)
                if scores and later(t, 1):
                    mask(t, 4, j % 2)
                if ahead and j == 0:
                    rest_of(s + 1, 1)
                if scores:
                    mask(t, 3, j % 2)
                if ahead and j == 0:
                    rest_of(s + 1, 2)
                if scores and later(t, 1):
                    mask(t, 6, j % 2)
                if scores:
                    mask(t, 7, j % 2)
                    mask(t, 5, j % 2)

            run(pool, start, step)

        @block.scalar
        def _(act):
            def x_t_copy(s, c, ps=None):
                act.wait_ge(s_xtr, s * DC + c + 1)
                if later(s, 1):
                    act.wait_ge(s_proj, s * NCH)
                nc.scalar.copy(x_t[:, c], (ps or proj_ps)[:, 0:SB]).then_inc(s_xt, 1)

            def proj_copy(s, m, ps=None):
                act.wait_ge(s_proj, s * NCH + m + 1)
                if later(s, 1):
                    act.wait_ge(s_lo, s * NCH - NCH + m + 1)
                    if m == 0:
                        act.wait_ge(s_vtr, s)
                nc.scalar.activation(proj[:, m], (ps or proj_ps)[:, 0:SB], ACT.Identity,
                                     bias=small_cols[:, BIAS_COL[m]:BIAS_COL[m] + 1]).then_inc(s_pcp, 1)

            def max_row_copy(t, j):
                act.wait_ge(s_maxtr, t + 1)
                if later(t, 2):
                    act.wait_ge(s_maxin, t * MAX_IN - MAX_IN)
                nc.scalar.copy(max_rows[0:PARTS * NTILE, j % 2],
                               max_ps[0][0:PARTS * NTILE, 0:P // 2].bitcast(BF16)).then_inc(s_maxrow, 1)

            def exps(t, i, buf):
                act.wait_ge(s_score, scored(t, i))
                if i <= 1 and later(t, 2):
                    act.wait_ge(s_av, t - 1)
                nc.scalar.activation(probs[:, buf, i], score_ps[i % 2][:, :], ACT.Exp, scale=SCALE).then_inc(s_exp, 1)

            def start():
                act.dma_start(bq_rows[:, :].rearrange("m (g r) -> m g r", g=GROUPS),
                              bq.rearrange("(g m r) -> m g r", g=GROUPS, m=QCH)).then_inc(s_small, 16)
                act.dma_start(small_rows[QCH:QCH + DC], mu_r.rearrange("(c p) -> c p", p=P)).then_inc(s_small, 16)
                act.dma_start(small_rows[QCH + DC:QCH + 2 * DC], mu_k.rearrange("(c p) -> c p", p=P)).then_inc(s_small, 16)
                act.dma_start(small_rows[N_COLS - 1:N_COLS, 0:DKV], bk.rearrange("(o n) -> o n", o=1)).then_inc(s_small, 16)
                act.dma_start(small_rows[N_COLS - 1:N_COLS, DKV:P], bv.rearrange("(o n) -> o n", o=1)).then_inc(s_small, 16)
                act.dma_start(bo_b[:, :], bo.rearrange("(o n) -> o n", o=1).to_broadcast([P, D])).then_inc(s_small, 16)
                act.wait_ge(s_const, 4)
                nc.scalar.activation(warm[:, :], minus_half[:, :], ACT.Exp)
                for c in range(DC):
                    x_t_copy(0, c, (gen0, gen1)[c])
                act.wait_ge(s_cols, 1)
                for m in range(NCH):
                    proj_copy(0, m, (proj_ps, max_ps[0], max_ps[1])[m])
                for n in range(3):
                    for c in range(DC):
                        act.wait_ge(s_wtr, DC * n + c + 1)
                        nc.scalar.copy(w_t[:, n, c], (gen0, gen1)[c][:, 0:D]).then_inc(s_wcp, 1)
                for c in range(DC):
                    x_t_copy(1, c)
                for m in range(NCH):
                    proj_copy(1, m)
                max_row_copy(0, 0)

            def step(s, j, par, project, coming, maxima, scores):
                t = s * SB_BLKS + j
                ahead = project and later(s, 1)
                f1, f2 = (behind(t, j, scores, n) for n in (1, 2))

                def att_t_copy():
                    act.wait_ge(s_av, t)
                    nc.scalar.copy(att_t[:, :], av_ps[:, :]).then_inc(s_att_t, 1)

                def x2_t_copy():
                    act.wait_ge(s_x2tr, t - 1)
                    if later(t, 4):
                        act.wait_ge(s_mix, (t - 3) * 4)
                    nc.scalar.copy(x2_t[:, (j - 2) % 2, :, 1:],
                                   gen0[:, 0:DC * BLK].rearrange("p (c q) -> p c q", q=BLK)).then_inc(s_x2t, 1)

                def att_c_copy():
                    act.wait_ge(s_ctr, t)
                    nc.scalar.copy(att_c[:, :, :],
                                   av_ps[:, 0:D].rearrange("p (c q) -> p c q", q=BLK)).then_inc(s_att_c, 1)

                def tanh():
                    act.wait_ge(s_r, t - 1)
                    nc.scalar.activation(tanh_r[:, :], gen1[:, 0:D], ACT.Tanh, scale=0.5).then_inc(s_tanh, 1)

                def relu():
                    act.wait_ge(s_k, t - 1)
                    nc.scalar.activation(relu_k[:, :, :], gen0[:, 0:DC * BLK].rearrange("p (c q) -> p c q", q=BLK),
                                         ACT.Relu).then_inc(s_relu, 1)

                def square():
                    act.wait_ge(s_relu, t - 1)
                    nc.scalar.activation(act_k[:, :, :], relu_k[:, :, :], ACT.Square).then_inc(s_act_k, 1)

                if scores and later(t, 1):
                    exps(t, 0, j % 2)
                if coming and j == 3:
                    x_t_copy(s + 2, 1)
                if scores:
                    exps(t, 1, j % 2)
                if scores and later(t, 1):
                    exps(t, 2, j % 2)
                if f1:
                    att_t_copy()
                if f2:
                    x2_t_copy()
                if coming and j == 3:
                    proj_copy(s + 2, 0)
                if scores:
                    exps(t, 3, j % 2)
                if scores and later(t, 1):
                    exps(t, 4, j % 2)
                if ahead and j == 0:
                    proj_copy(s + 1, 1)
                if maxima:
                    max_row_copy(t + 1, j + 1)
                if scores:
                    exps(t, 5, j % 2)
                if f1:
                    att_c_copy()
                if f2:
                    tanh()
                if ahead and j == 0:
                    proj_copy(s + 1, 2)
                if coming and j == 2:
                    x_t_copy(s + 2, 0)
                if scores and later(t, 1):
                    exps(t, 6, j % 2)
                if scores:
                    exps(t, 7, j % 2)
                if f2:
                    relu()
                    square()

            run(act, start, step)

        @block.vector
        def _(dve):
            def hi(s, m):
                dve.wait_ge(s_pcp, s * NCH + m + 1)
                if later(s, 1):
                    if m:
                        dve.wait_ge(s_spill_q, s * SPILLS)
                    else:
                        dve.wait_ge(s_spill_k, s * 16)
                nc.vector.tensor_copy(parts[:, m, 0], proj[:, m]).then_inc(s_hi, 1)

            def mid_lo(s, m):
                dve.wait_ge(s_rest, s * NCH + m + 1)
                nc.vector.tensor_copy(parts[:, m, 1], rest[:, m]).then_inc(s_mid, 1)
                dve.wait_ge(s_mid, s * NCH + m + 1)
                nc.vector.tensor_tensor(parts[:, m, 2], rest[:, m], parts[:, m, 1], ALU.subtract).then_inc(s_lo, 1)

            def val_copy(s, par):
                dve.wait_ge(s_vtr, s + 1)
                if later(s, 2):
                    dve.wait_ge(s_av, s * SB_BLKS - 3)
                nc.vector.tensor_copy(vals[:, par, :, :, 0:DH],
                                      proj_ps[:, 0:SB].rearrange("p (j x g d) -> p j x g d", x=2, g=GROUPS, d=DH)[:, :, 1]
                                      ).then_inc(s_val, 1)

            def tile_q(t, s, j, par):
                if j == 0:
                    dve.wait_ge(s_stack, s * STACKS + STACKS)
                nc.vector.tensor_copy(q_tiles[:, j % 2].rearrange("r n (h q) -> r n h q", q=SUB),
                                      qs[0:ROWS, par, j].rearrange("r h g (n q) -> r (g n) h q", q=SUB)
                                      ).then_inc(s_tiles, 1)

            def tile_max(t, j, i):
                n = min(TPB, NTILE - TPB * i)
                dve.wait_ge(s_maxsc, t * NMAXB + i + 1)
                nc.vector.tensor_reduce(neg_max[:, TPB * i:TPB * i + n],
                                        max_bank(t, j, i)[:, 0:n * TILE_KEYS].rearrange("p (n k) -> p n k", k=TILE_KEYS),
                                        AX_X, ALU.max, negate=True).then_inc(s_max, 1)

            def cut_max(t, j):
                mp = max_parts[:, j % 2]
                dve.wait_ge(s_max, t * NMAXB + NMAXB)
                nc.vector.tensor_copy(mp[:, 0], neg_max[:, :]).then_inc(s_mx, 1)
                dve.wait_ge(s_mx, t * 4 + 1)
                nc.vector.tensor_tensor(max_rest[:, :], neg_max[:, :], mp[:, 0], ALU.subtract).then_inc(s_mx, 1)
                dve.wait_ge(s_mx, t * 4 + 2)
                nc.vector.tensor_copy(mp[:, 1], max_rest[:, :]).then_inc(s_mx, 1)
                dve.wait_ge(s_mx, t * 4 + 3)
                nc.vector.tensor_tensor(mp[:, 2], max_rest[:, :], mp[:, 1], ALU.subtract).then_inc(s_mx, 1)

            def moments(u, y, y_done, stats, mv, var, done):
                dve.wait_ge(y_done, u + 1)
                nc.vector.bn_stats(stats[:, :], y[:, :]).then_inc(done, 1)
                dve.wait_ge(done, u * 3 + 1)
                dve.nop(nofuse=True)
                nc.vector.bn_aggr(mv[:, :], stats[:, :]).then_inc(done, 1)
                dve.wait_ge(done, u * 3 + 2)
                nc.vector.tensor_scalar(var[:, :], mv[:, 1:2], EPS, None, ALU.add).then_inc(done, 1)

            def start():
                dve.wait_ge(s_small, N_SMALL)
                nc.vector.tensor_copy(small_rows[0:QCH].rearrange("m (d h g) -> m d h g", d=DH, g=GROUPS),
                                      bq_rows[:, :].rearrange("m (g h d) -> m d h g", g=GROUPS, d=DH)).then_inc(s_bqp, 1)
                dve.wait_ge(s_wq, 16)
                for c in range(DC):
                    for m in range(QCH):
                        nc.vector.tensor_copy(
                            wqkv[:, c, (1 + m) * P:(2 + m) * P].rearrange("p (d h g) -> p d h g", d=DH, g=GROUPS),
                            wq_raw[:, c].rearrange("p (g m h d) -> p m d h g", g=GROUPS, m=QCH, d=DH)[:, m]
                        ).then_inc(s_wqp, 1)
                dve.wait_ge(s_smalltr, 1)
                nc.vector.tensor_copy(small_cols[:, :], score_ps[0][:, 0:N_COLS]).then_inc(s_cols, 1)
                dve.wait_ge(s_cols, 1)
                nc.vector.memset(ks[0:ROWS, 0, :, 0:WINDOW], 0.0).then_inc(s_zero, 1)
                nc.vector.memset(vals[:, :, :, :, DH:DH + 1], 1.0).then_inc(s_zero, 1)
                nc.vector.memset(vals[:, :, :, :, DH + 1:], 0.0).then_inc(s_zero, 1)
                nc.vector.memset(x2_t[:, 0, :, 0:1], 0.0).then_inc(s_zero, 1)
                for buf in range(2):
                    nc.vector.memset(out_t[:, buf, 0:1], 0.0).then_inc(s_store[buf], 1)
                dve.wait_ge(s_ident, 1)
                nc.vector.tensor_copy(ident_b[:, :], ident[:, :]).then_inc(s_masks, 1)
                for m in range(NCH):
                    hi(0, m)
                    if m:
                        mid_lo(0, m - 1)
                mid_lo(0, NCH - 1)
                val_copy(0, 0)
                dve.wait_ge(s_edge, 16 * 2 * (HPG - 1))
                for n in range(TPB):
                    nc.vector.tensor_copy(edge_mask[:, n], edge_f[:, :, :]).then_inc(s_masks, 1)
                nc.vector.tensor_copy(first_mask[:, :, :], first_f[:, :, :]).then_inc(s_masks, 1)
                hi(1, 0)
                mid_lo(1, 0)
                hi(1, 1)
                tile_q(0, 0, 0, 0)
                tile_q(1, 0, 1, 0)
                for i in range(NMAXB):
                    tile_max(0, 0, i)
                cut_max(0, 0)
                mid_lo(1, 1)
                hi(1, 2)
                mid_lo(1, 2)
                val_copy(1, 1)

            def step(s, j, par, project, coming, maxima, scores):
                t = s * SB_BLKS + j
                ahead = project and later(s, 1)
                f1, f2, f3 = (behind(t, j, scores, n) for n in (1, 2, 3))
                jv, pv = at(j, par, -1)
                u2, u3 = (j - 2) % 2, (j - 3) % 2

                def mixed(w):
                    dve.wait_ge(s_diff, t - 1)
                    if later(t, 3):
                        dve.wait_ge(s_k if w else s_r, t - 2)
                    for c in range(DC):
                        nc.vector.scalar_tensor_tensor(
                            out=mix[:, w, c], in0=diff[:, c],
                            scalar=small_cols[:, MU_COL + w * DC + c:MU_COL + w * DC + c + 1],
                            in1=x2_t[:, u2, c, 0:BLK], op0=ALU.mult, op1=ALU.add).then_inc(s_mix, 1)

                def first_norm():
                    dve.wait_ge(s_rstd1, t - 1)
                    if later(t, 4):
                        dve.wait_ge(s_x2tr, t - 3)
                    nc.vector.tensor_scalar(x2[:, u2], y1[:, :], mv1[:, 0:1], rstd1[:, 0:1],
                                            ALU.subtract, ALU.mult).then_inc(s_x2, 1)

                def token_before():
                    if later(t, 3):
                        dve.wait_ge(s_x2t, t - 2)
                        nc.vector.tensor_copy(x2_t[:, u2, :, 0:1],
                                              x2_t[:, 1 - u2, :, BLK:BLK + 1]).then_inc(s_x2p, 1)

                def gate():
                    dve.wait_ge(s_v, t - 2)
                    dve.wait_ge(s_tanh, t - 2)
                    nc.vector.scalar_tensor_tensor(out=gated[:, :], in0=tanh_r[:, :], scalar=1.0,
                                                   in1=gen0[:, 0:D], op0=ALU.add, op1=ALU.mult).then_inc(s_gated, 1)

                def second_residual():
                    dve.wait_ge(s_gated, t - 2)
                    nc.vector.scalar_tensor_tensor(out=y2[:, :], in0=gated[:, :], scalar=0.5,
                                                   in1=x2[:, u3], op0=ALU.mult, op1=ALU.add).then_inc(s_y2, 1)
                    moments(t - 3, y2, s_y2, stats2, mv2, var2, s_ln2)

                def normalise():
                    dve.wait_ge(s_atr, t)
                    acc = gen1[:, :].rearrange("p (h g v) -> p h g v", h=HPG, v=VCOL)
                    rc = recip[:, :].rearrange("p (h g v) -> p h g v", h=HPG, v=1)
                    nc.vector.reciprocal(rc, acc[:, :, :, DH:DH + 1]).then_inc(s_recip, 1)
                    dve.wait_ge(s_recip, t)
                    if later(t, 2):
                        dve.wait_ge(s_ctr, t - 1)
                    nc.vector.tensor_tensor(att[:, :].rearrange("p (g h v) -> p h g v", g=GROUPS, v=DH),
                                            acc[:, :, :, 0:DH], rc.to_broadcast([P, HPG, GROUPS, DH]),
                                            ALU.mult).then_inc(s_att, 1)

                def second_norm():
                    dve.wait_ge(s_rstd2, t - 2)
                    if later(t, 5):
                        dve.wait_ge(s_store[u3], stored(s, j))
                    nc.vector.tensor_scalar(out_t[:, u3], y2[:, :], mv2[:, 0:1], rstd2[:, 0:1],
                                            ALU.subtract, ALU.mult).then_inc(s_out, 1)

                def tiles_ahead():
                    jn, pn = at(j, par, 2)
                    tile_q(t + 2, s if j < SB_BLKS - 2 else s + 1, jn, pn)

                def first_residual():
                    dve.wait_ge(s_wo_ps, t)
                    if not later(t, 5):
                        dve.wait_ge(s_xbo, 1)
                    else:
                        dve.wait_ge(s_xbo, s + 1 if j else s)
                    nc.vector.tensor_tensor(y1[:, :], gen1[:, 0:D], x_bo[:, pv, jv], ALU.add).then_inc(s_y1, 1)
                    moments(t - 1, y1, s_y1, stats1, mv1, var1, s_ln1)

                if maxima:
                    tile_max(t + 1, (j + 1) % SB_BLKS, 0)
                    tile_max(t + 1, (j + 1) % SB_BLKS, 1)
                    tile_max(t + 1, (j + 1) % SB_BLKS, 2)
                if f2:
                    token_before()
                if ahead and j == 1:
                    mid_lo(s + 1, 2)
                if f2:
                    first_norm()
                if f3:
                    gate()
                if maxima:
                    tile_max(t + 1, (j + 1) % SB_BLKS, 3)
                if f3:
                    second_residual()
                if maxima:
                    tile_max(t + 1, (j + 1) % SB_BLKS, 4)
                    tile_max(t + 1, (j + 1) % SB_BLKS, 5)
                    cut_max(t + 1, j + 1)
                if f1:
                    normalise()
                if f2:
                    mixed(0)
                    mixed(1)
                if coming and j == 3:
                    hi(s + 2, 0)
                if maxima and (project or j < SB_BLKS - 2):
                    tiles_ahead()
                if ahead and j == 0:
                    hi(s + 1, 1)
                if f3:
                    second_norm()
                if coming and j == 3:
                    mid_lo(s + 2, 0)
                if ahead and j == 0:
                    mid_lo(s + 1, 1)
                if ahead and j == 1:
                    val_copy(s + 1, 1 - par)
                if ahead and j == 0:
                    hi(s + 1, 2)
                if f1:
                    first_residual()

            run(dve, start, step)

        @block.tensor
        def _(pe):
            def x_turn(s, c, ps=None):
                if c == 0:
                    pe.wait_ge(s_x, s * 16 + 16)
                    if later(s, 1):
                        pe.wait_ge(s_val, s)
                    if later(s, 2):
                        pe.wait_ge(s_max, (s - 1) * SB_BLKS * NMAXB)
                elif ps is None:
                    pe.wait_ge(s_xt, s * DC + 1)
                for b in range(SB_BLKS):
                    ins = nc.tensor.transpose((ps or proj_ps)[:, b * BLK:(b + 1) * BLK], x_in[:, b, c * P:(c + 1) * P],
                                              ident[:, :])
                ins.then_inc(s_xtr, 1)

            def project_chunk(s, m, ps=None):
                if m == 0:
                    pe.wait_ge(s_xt, s * DC + DC)
                elif ps is None:
                    pe.wait_ge(s_pcp, s * NCH + m)
                    if m == 1 and later(s, 2):
                        pe.wait_ge(s_max, ((s - 1) * SB_BLKS + 2) * NMAXB)
                for c in range(DC):
                    ins = nc.tensor.matmul((ps or proj_ps)[:, 0:SB], wqkv[:, c, m * P:(m + 1) * P], x_t[:, c],
                                           start=(c == 0), stop=(c == DC - 1))
                ins.then_inc(s_proj, 1)

            def v_turn(s):
                pe.wait_ge(s_pcp, s * NCH + NCH)
                if later(s, 2):
                    pe.wait_ge(s_max, ((s - 1) * SB_BLKS + 3) * NMAXB)
                for b in range(SB_BLKS):
                    ins = nc.tensor.transpose(proj_ps[:, b * BLK:(b + 1) * BLK],
                                              proj[:, 0, b * BLK:(b + 1) * BLK], ident[:, :])
                ins.then_inc(s_vtr, 1)

            def max_scores(t, j, par, i, s=0, project=False):
                if i == 0:
                    pe.wait_ge(s_tiles, t + 1)
                    if later(t, 1):
                        pe.wait_ge(s_maxrow, t)
                elif j in THREE_BANKS and later(t, 1):
                    if i == 2:
                        if project and later(s, 1) and j == 1:
                            pe.wait_ge(s_pcp, s * NCH + NCH + 1)
                        elif project and later(s, 1) and j == 2:
                            pe.wait_ge(s_pcp, s * NCH + 2 * NCH)
                        else:
                            pe.wait_ge(s_val, s + 2 if project else s + 1)
                    elif i > 2:
                        pe.wait_ge(s_max, t * NMAXB + i - 2)
                elif i >= 2:
                    pe.wait_ge(s_max, t * NMAXB + i - 1)
                tiles = range(TPB * i, min(TPB * (i + 1), NTILE))
                out_ps = max_bank(t, j, i)[:, 0:len(tiles) * TILE_KEYS]
                if later(t, 1):
                    edges = out_ps.rearrange("p (n e k) -> p n e k", n=len(tiles), k=SUB)[:, :, 0::TILE_KEYS // SUB - 1, :]
                    nc.tensor.matmul(edges, ident_b[:, :], edge_mask[:, 0:len(tiles)], start=True, stop=False,
                                     skip_group_check=True)
                for k, tile in enumerate(tiles):
                    g, n = tile // NSUB, tile % NSUB
                    dst = out_ps[:, k * TILE_KEYS:(k + 1) * TILE_KEYS]
                    if not later(t, 1):
                        nc.tensor.matmul(dst, ident_b[:, :], first_mask[:, n], start=(k == 0), stop=False,
                                         skip_group_check=True)
                    k0 = j * BLK + n * SUB
                    ins = nc.tensor.matmul(dst, q_tiles[:, j % 2, tile],
                                           ks[0:ROWS, par, g, k0:k0 + TILE_KEYS], start=False,
                                           stop=(k == len(tiles) - 1), skip_group_check=True)
                ins.then_inc(s_maxsc, 1)

            def max_turn(t, j):
                pe.wait_ge(s_mx, t * 4 + 4)
                pe.nop(nofuse=True)
                nc.tensor.transpose(max_ps[0][0:PARTS * NTILE, 0:P // 2].bitcast(BF16),
                                    max_parts[:, j % 2].rearrange("p a n -> p (a n)"), ident_b[:, :]).then_inc(s_maxtr, 1)

            def score(t, j, par, i):
                g = i // 2
                if i == 0 or (i == 1 and not later(t, 1)):
                    pe.wait_ge(s_maxin, t * MAX_IN + MAX_IN)
                if later(t, 1):
                    pe.wait_ge(s_exp, scored(t, i) - 2)
                elif i > 1:
                    pe.wait_ge(s_exp, scored(t, i) - 1)
                k0 = j * BLK + (WINDOW if i % 2 else 0)
                nc.tensor.matmul(score_ps[i % 2][:, :].rearrange("p (h q) -> p h q", q=BLK),
                                 ks[0:ROWS + PARTS, par, g, k0:k0 + BLK], qs[0:ROWS + PARTS, par, j, :, g, :],
                                 start=True, stop=True).then_inc(s_score, 1)

            def values(t, j, par):
                pe.wait_ge(s_prob, scored(t, NSCORE - 1))
                if later(t, 1):
                    pe.wait_ge(s_att_c, t)
                halves = (0, 1) if later(t, 1) else (1,)
                for half in halves:
                    jk, pk = at(j, par, half - 1)
                    for g in range(GROUPS):
                        ins = nc.tensor.matmul(av_ps[g * VCOL:(g + 1) * VCOL, :], vals[:, pk, jk, g, :],
                                               probs[:, j % 2, 2 * g + half], start=(half == halves[0]),
                                               stop=(half == 1), skip_group_check=True)
                ins.then_inc(s_av, 1)

            def start():
                pe.wait_ge(s_ident, 1)
                for c in range(DC):
                    x_turn(0, c, (gen0, gen1)[c])
                pe.wait_ge(s_small, N_SMALL)
                pe.wait_ge(s_bqp, 1)
                nc.tensor.transpose(score_ps[0][:, 0:N_COLS], small_rows[:, :], ident[0:N_COLS, 0:N_COLS]).then_inc(s_smalltr, 1)
                pe.wait_ge(s_wkv, 32)
                for m in range(NCH):
                    if m == 1:
                        pe.wait_ge(s_wqp, DC * QCH)
                    project_chunk(0, m, (proj_ps, max_ps[0], max_ps[1])[m])
                v_turn(0)
                pe.wait_ge(s_wffn, 48)
                pe.wait_ge(s_wo, 16)
                for n in range(3):
                    for c in range(DC):
                        if n:
                            pe.wait_ge(s_wcp, DC * (n - 1) + c + 1)
                        for o in range(DC):
                            ins = nc.tensor.transpose((gen0, gen1)[c][:, o * P:(o + 1) * P],
                                                      w_raw[:, n, o, c * P:(c + 1) * P], ident[:, :])
                        ins.then_inc(s_wtr, 1)
                for c in range(DC):
                    x_turn(1, c)
                for m in range(QCH):
                    project_chunk(1, m)
                pe.wait_ge(s_zero, 4)
                pe.wait_ge(s_const, N_CONST + 1)
                pe.wait_ge(s_masks, 2 + TPB)
                for i in range(NMAXB):
                    max_scores(0, 0, 0, i)
                    if i == 1:
                        project_chunk(1, QCH)
                max_turn(0, 0)
                v_turn(1)
                pe.wait_ge(s_wcp, 3 * DC)

            def step(s, j, par, project, coming, maxima, scores):
                t = s * SB_BLKS + j
                ahead = project and later(s, 1)
                f1, f2, f3 = (behind(t, j, scores, n) for n in (1, 2, 3))
                jn, pn = at(j, par, 1)
                jv, pv = at(j, par, -1)
                u2 = (j - 2) % 2

                def second_product():
                    pe.wait_ge(s_act_k, t - 2)
                    for c in range(DC):
                        ins = nc.tensor.matmul(gen0[:, 0:D], act_k[:, c], w_t[:, 2, c], start=(c == 0),
                                               stop=(c == DC - 1))
                    ins.then_inc(s_v, 1)

                def turn_x2():
                    pe.wait_ge(s_x2, t - 1)
                    if f3:
                        pe.wait_ge(s_gated, t - 2)
                    for c in range(DC):
                        ins = nc.tensor.transpose(gen0[:, c * BLK:(c + 1) * BLK], x2[:, u2, c * P:(c + 1) * P],
                                                  ident[:, :])
                    ins.then_inc(s_x2tr, 1)

                def turn_back():
                    pe.wait_ge(s_att_t, t)
                    if later(t, 2):
                        pe.wait_ge(s_y1, t - 1)
                    for h in range(HPG):
                        ins = nc.tensor.transpose(gen1[:, h * P:(h + 1) * P], att_t[:, h * BLK:(h + 1) * BLK],
                                                  ident[:, :])
                    ins.then_inc(s_atr, 1)

                def turn_attention():
                    pe.wait_ge(s_att, t)
                    for c in range(DC):
                        ins = nc.tensor.transpose(av_ps[:, c * BLK:(c + 1) * BLK], att[:, c * P:(c + 1) * P],
                                                  ident[:, :])
                    ins.then_inc(s_ctr, 1)

                def r_product():
                    pe.wait_ge(s_mix, (t - 2) * 4 + 2)
                    if f1:
                        pe.wait_ge(s_att, t)
                    else:
                        pe.wait_ge(s_y1, t - 1)
                    for c in range(DC):
                        ins = nc.tensor.matmul(gen1[:, 0:D], mix[:, 0, c], w_t[:, 0, c], start=(c == 0),
                                               stop=(c == DC - 1))
                    ins.then_inc(s_r, 1)

                def k_product():
                    pe.wait_ge(s_mix, (t - 2) * 4 + 4)
                    pe.wait_ge(s_x2t, t - 1)
                    for o in range(DC):
                        for c in range(DC):
                            ins = nc.tensor.matmul(gen0[:, o * BLK:(o + 1) * BLK], w_t[:, 1, c, o * P:(o + 1) * P],
                                                   mix[:, 1, c], start=(c == 0), stop=(c == DC - 1))
                    ins.then_inc(s_k, 1)

                def output_product():
                    pe.wait_ge(s_att_c, t)
                    if f2:
                        pe.wait_ge(s_tanh, t - 1)
                    for c in range(DC):
                        ins = nc.tensor.matmul(gen1[:, 0:D], att_c[:, c], wo[:, c], start=(c == 0),
                                               stop=(c == DC - 1))
                    ins.then_inc(s_wo_ps, 1)

                if maxima:
                    max_scores(t + 1, jn, pn, 0, s, project)
                    max_scores(t + 1, jn, pn, 1, s, project)
                if scores and later(t, 1):
                    score(t, j, par, 0)
                if coming and j == 3:
                    x_turn(s + 2, 1)
                if maxima:
                    max_scores(t + 1, jn, pn, 2, s, project)
                if scores:
                    score(t, j, par, 1)
                if f3:
                    second_product()
                if maxima:
                    max_scores(t + 1, jn, pn, 3, s, project)
                if f1:
                    values(t - 1, jv, pv)
                if scores and later(t, 1):
                    score(t, j, par, 2)
                if maxima:
                    max_scores(t + 1, jn, pn, 4, s, project)
                if f2:
                    turn_x2()
                if maxima:
                    max_scores(t + 1, jn, pn, 5, s, project)
                if scores:
                    score(t, j, par, 3)
                if coming and j == 3:
                    project_chunk(s + 2, 0)
                if scores and later(t, 1):
                    score(t, j, par, 4)
                if f1:
                    turn_back()
                if ahead and j == 0:
                    project_chunk(s + 1, 1)
                if scores:
                    score(t, j, par, 5)
                if maxima:
                    max_turn(t + 1, j + 1)
                if ahead and j == 1:
                    v_turn(s + 1)
                if f1:
                    turn_attention()
                if scores and later(t, 1):
                    score(t, j, par, 6)
                if f2:
                    r_product()
                if ahead and j == 0:
                    project_chunk(s + 1, 2)
                if scores:
                    score(t, j, par, 7)
                if coming and j == 2:
                    x_turn(s + 2, 0)
                if f1:
                    output_product()
                if f2:
                    k_product()

            run(pe, start, step)


_INS = ['L0_attn_x', 'L0_attn_Wq', 'L0_attn_bq', 'L0_attn_Wk', 'L0_attn_bk', 'L0_attn_Wv', 'L0_attn_bv', 'L0_attn_Wo',
        'L0_attn_bo', 'L0_ffn_W_r', 'L0_ffn_W_k', 'L0_ffn_W_v', 'L0_ffn_mu_r', 'L0_ffn_mu_k']


def kernel(**inputs):
    import numpy as np
    import concourse.bacc as bacc
    from concourse.bass_utils import run_bass_kernel_spmd

    nc = bacc.Bacc("TRN2", target_bir_lowering=False, num_devices=1)
    arrays, args = {}, []
    for name in _INS:
        a = np.ascontiguousarray(inputs[name])
        arrays[f"in_{name}"] = a
        args.append(nc.dram_tensor(f"in_{name}", a.shape, mybir.dt.from_np(a.dtype), kind="ExternalInput").ap())
    shape = inputs['L0_attn_x'].shape
    args.append(nc.dram_tensor("out_0", shape, F32, kind="ExternalOutput").ap())
    attention_channel_mix(nc, *args)
    r = run_bass_kernel_spmd(nc, [arrays], core_ids=[0])
    return r.results[0]["out_0"]
```
